# Optimizing a Trainium2 kernel written in Bass

```python
import numpy as np
import jax
import jax.numpy as jnp

def _softmax(x, axis=-1):
    return jax.nn.softmax(x, axis=axis)

def _gelu(x):
    return jax.nn.gelu(x, approximate=True)

def _silu(x):
    return jax.nn.silu(x)

def _sigmoid(x):
    return jax.nn.sigmoid(x)

def _layernorm(x, axis=-1, eps=1e-05):
    m = jnp.mean(x, axis=axis, keepdims=True)
    v = jnp.var(x, axis=axis, keepdims=True)
    return (x - m) / jnp.sqrt(v + eps)

def _scatter_add(tgt, idx, src, axis=0):
    return tgt.at[idx].add(src)

def _segment_sum(src, seg, n):
    return jax.ops.segment_sum(src, seg, n)
kernel_name = 'mk_cond_resid_d2_seqx_r8_126c0f'

def setup_inputs(seed: int=0):
    np.random.seed(seed)
    _w = jnp.asarray

    def _rec_inputs():
        import jax
        import jax.numpy as jnp
        _rk = jax.random.key(seed)
        x = -0.000125 + 0.9999 * jax.random.normal(jax.random.fold_in(_rk, 1), (8, 128, 512), jnp.float32)
        _lenS = 128 - jax.random.randint(jax.random.fold_in(_rk, 7), (8,), 0, max(1, 128 // 4) + 1, jnp.int32)
        _lenS2 = 128 - jax.random.randint(jax.random.fold_in(_rk, 8), (8,), 0, max(1, 128 // 4) + 1, jnp.int32)
        itok_B_0_7 = jax.random.randint(jax.random.fold_in(_rk, 11), (8,), 0, 8, jnp.int32)
        itok_Bx16_0_63 = jax.random.randint(jax.random.fold_in(_rk, 12), (8, 16), 0, 64, jnp.int32)
        itok_B_207_1644 = jax.random.randint(jax.random.fold_in(_rk, 13), (8,), 207, 1645, jnp.int32)
        return (x, itok_B_0_7, itok_Bx16_0_63, itok_B_207_1644)
    x, itok_B_0_7, itok_Bx16_0_63, itok_B_207_1644 = _rec_inputs()

    def _L0_cond_setup():
        import jax, jax.numpy as jnp
        import numpy as np
        TOP_K = 2
        LANG_BIAS = 5.0
        SCALING = 32.0 / 16.0
        LANGUAGE_PAD_ID = -1
        key = jax.random.key(seed)
        ks = jax.random.split(key, 6)
        B, T, D, O, E, R = (4, 256, 512, 512, 8, 16)
        x = jax.random.normal(ks[0], (B, T, D), dtype=jnp.float32)
        language_ids = jax.random.randint(ks[1], (B,), 0, E).astype(jnp.int64)
        W = jax.random.normal(ks[2], (O, D), dtype=jnp.float32) * (1.0 / np.sqrt(D))
        Wr = jax.random.normal(ks[3], (E, D), dtype=jnp.float32) * (1.0 / np.sqrt(D))
        A = jax.random.normal(ks[4], (E, R, D), dtype=jnp.float32) * (1.0 / np.sqrt(D))
        Bm = jax.random.normal(ks[5], (O, R), dtype=jnp.float32) * 0.0
        Bm = jnp.broadcast_to(Bm, (E, O, R)) + jax.random.normal(ks[5], (E, O, R), dtype=jnp.float32) * 0.02
        return {'x': x, 'language_ids': language_ids, 'W': W, 'Wr': Wr, 'A': A, 'B': Bm}
    _L0_cond_all = _L0_cond_setup()
    _L0_cond_in = {k: v for k, v in _L0_cond_all.items() if k in ('W', 'Wr', 'A', 'B')}
    del _L0_cond_all

    def _L1_cond_setup():
        import jax, jax.numpy as jnp
        import numpy as np
        B, S, HID = (4, 128, 512)
        D, HQ, HK = (128, 32, 8)
        PAGES, PSIZE, NPP = (64, 32, 16)
        THETA = 10000.0
        EPS = 1e-06
        SCALE = 1.0 / float(np.sqrt(D))

        def _rmsnorm(t, w):
            var = jnp.mean(t * t, axis=-1, keepdims=True)
            return t * jax.lax.rsqrt(var + EPS) * w

        def _rope(t, pos):
            inv_freq = 1.0 / THETA ** (jnp.arange(0, D, 2, dtype=jnp.float32) / D)
            freqs = pos[..., None].astype(jnp.float32) * inv_freq
            cos = jnp.cos(freqs)[:, :, None, :]
            sin = jnp.sin(freqs)[:, :, None, :]
            t1, t2 = (t[..., :D // 2], t[..., D // 2:])
            return jnp.concatenate([t1 * cos - t2 * sin, t2 * cos + t1 * sin], axis=-1)
        key = jax.random.key(seed)
        ks = jax.random.split(key, 10)
        x = jax.random.normal(ks[0], (B, S, HID), jnp.float32)
        Wq = jax.random.normal(ks[1], (HQ * D, HID), jnp.float32) * 0.02
        Wk = jax.random.normal(ks[2], (HK * D, HID), jnp.float32) * 0.02
        Wv = jax.random.normal(ks[3], (HK * D, HID), jnp.float32) * 0.02
        Wo = jax.random.normal(ks[4], (HID, HQ * D), jnp.float32) * 0.02
        q_norm_w = jax.random.uniform(ks[5], (D,), jnp.float32)
        k_norm_w = jax.random.uniform(ks[6], (D,), jnp.float32)
        k_cache = jax.random.normal(ks[7], (PAGES, PSIZE, HK, D), jnp.float32)
        v_cache = jax.random.normal(ks[8], (PAGES, PSIZE, HK, D), jnp.float32)
        block_table = jnp.arange(B * NPP, dtype=jnp.int32).reshape(B, NPP)
        cache_seqlens = jax.random.randint(ks[9], (B,), 0, 475).astype(jnp.int32)
        return dict(x=x, Wq=Wq, Wk=Wk, Wv=Wv, Wo=Wo, q_norm_w=q_norm_w, k_norm_w=k_norm_w, k_cache=k_cache, v_cache=v_cache, block_table=block_table, cache_seqlens=cache_seqlens)
    _L1_cond_all = _L1_cond_setup()
    _L1_cond_in = {k: v for k, v in _L1_cond_all.items() if k in ('Wq', 'Wk', 'Wv', 'Wo', 'q_norm_w', 'k_norm_w', 'k_cache', 'v_cache')}
    del _L1_cond_all
    return {'x': x, 'itok_B_0_7': itok_B_0_7, 'itok_Bx16_0_63': itok_Bx16_0_63, 'itok_B_207_1644': itok_B_207_1644, 'L0_cond_W': _L0_cond_in['W'], 'L0_cond_Wr': _L0_cond_in['Wr'], 'L0_cond_A': _L0_cond_in['A'], 'L0_cond_B': _L0_cond_in['B'], 'L1_cond_Wq': _L1_cond_in['Wq'], 'L1_cond_Wk': _L1_cond_in['Wk'], 'L1_cond_Wv': _L1_cond_in['Wv'], 'L1_cond_Wo': _L1_cond_in['Wo'], 'L1_cond_q_norm_w': _L1_cond_in['q_norm_w'], 'L1_cond_k_norm_w': _L1_cond_in['k_norm_w'], 'L1_cond_k_cache': _L1_cond_in['k_cache'], 'L1_cond_v_cache': _L1_cond_in['v_cache']}

def reference(x, itok_B_0_7, itok_Bx16_0_63, itok_B_207_1644, L0_cond_W, L0_cond_Wr, L0_cond_A, L0_cond_B, L1_cond_Wq, L1_cond_Wk, L1_cond_Wv, L1_cond_Wo, L1_cond_q_norm_w, L1_cond_k_norm_w, L1_cond_k_cache, L1_cond_v_cache):
    import jax
    import jax.numpy as jnp

    def _L0_cond_ref(x, language_ids, W, Wr, A, B):
        import jax, jax.numpy as jnp
        import numpy as np
        TOP_K = 2
        LANG_BIAS = 5.0
        SCALING = 32.0 / 16.0
        LANGUAGE_PAD_ID = -1
        base = jnp.einsum('btd,od->bto', x, W)
        E = Wr.shape[0]
        logits = jnp.einsum('btd,ed->bte', x.astype(jnp.float32), Wr.astype(jnp.float32))
        expert_targets = language_ids
        valid = expert_targets >= 0
        tgt = jnp.where(valid, expert_targets, 0)
        bias = jax.nn.one_hot(tgt, E, dtype=logits.dtype) * LANG_BIAS
        bias = jnp.where(valid[:, None], bias, 0.0)
        logits = logits + bias[:, None, :]
        topw, topi = jax.lax.top_k(logits, TOP_K)
        weights = jax.nn.softmax(topw, axis=-1)
        gates = jnp.sum(jax.nn.one_hot(topi, E, dtype=weights.dtype) * weights[..., None], axis=-2)
        gates = gates.astype(x.dtype)
        h = jnp.einsum('btd,erd->bter', x, A)
        lora_out = jnp.einsum('bter,bte,eor->bto', h, gates, B)
        return base + SCALING * lora_out

    def _L1_cond_ref(x, Wq, Wk, Wv, Wo, q_norm_w, k_norm_w, k_cache, v_cache, block_table, cache_seqlens):
        import jax, jax.numpy as jnp
        import numpy as np
        B, S, HID = (4, 128, 512)
        D, HQ, HK = (128, 32, 8)
        PAGES, PSIZE, NPP = (64, 32, 16)
        THETA = 10000.0
        EPS = 1e-06
        SCALE = 1.0 / float(np.sqrt(D))

        def _rmsnorm(t, w):
            var = jnp.mean(t * t, axis=-1, keepdims=True)
            return t * jax.lax.rsqrt(var + EPS) * w

        def _rope(t, pos):
            inv_freq = 1.0 / THETA ** (jnp.arange(0, D, 2, dtype=jnp.float32) / D)
            freqs = pos[..., None].astype(jnp.float32) * inv_freq
            cos = jnp.cos(freqs)[:, :, None, :]
            sin = jnp.sin(freqs)[:, :, None, :]
            t1, t2 = (t[..., :D // 2], t[..., D // 2:])
            return jnp.concatenate([t1 * cos - t2 * sin, t2 * cos + t1 * sin], axis=-1)
        bsz, seqlen, _ = x.shape
        q = jnp.einsum('bsd,ed->bse', x, Wq).reshape(bsz, seqlen, HQ, D)
        k = jnp.einsum('bsd,ed->bse', x, Wk).reshape(bsz, seqlen, HK, D)
        v = jnp.einsum('bsd,ed->bse', x, Wv).reshape(bsz, seqlen, HK, D)
        q = _rmsnorm(q, q_norm_w)
        k = _rmsnorm(k, k_norm_w)
        pos = cache_seqlens[:, None] + jnp.arange(seqlen)[None, :]
        q = _rope(q, pos)
        k = _rope(k, pos)
        L = NPP * PSIZE
        kc = k_cache[block_table].reshape(bsz, L, HK, D)
        vc = v_cache[block_table].reshape(bsz, L, HK, D)
        k_all = jnp.concatenate([kc, k], axis=1)
        v_all = jnp.concatenate([vc, v], axis=1)
        valid_c = jnp.arange(L)[None, :] < cache_seqlens[:, None]
        valid = jnp.concatenate([valid_c, jnp.ones((bsz, seqlen), dtype=bool)], axis=1)
        rep = HQ // HK
        k_all = jnp.repeat(k_all, rep, axis=2)
        v_all = jnp.repeat(v_all, rep, axis=2)
        scores = jnp.einsum('bqhd,bkhd->bhqk', q, k_all) * SCALE
        scores = jnp.where(valid[:, None, None, :], scores, -1e+30)
        probs = jax.nn.softmax(scores, axis=-1)
        o = jnp.einsum('bhqk,bkhd->bqhd', probs, v_all)
        o = o.reshape(bsz, seqlen, HQ * D)
        return jnp.einsum('bse,de->bsd', o, Wo)
    x = x + _L0_cond_ref(x, itok_B_0_7, L0_cond_W, L0_cond_Wr, L0_cond_A, L0_cond_B)
    x = x + _L1_cond_ref(x, L1_cond_Wq, L1_cond_Wk, L1_cond_Wv, L1_cond_Wo, L1_cond_q_norm_w, L1_cond_k_norm_w, L1_cond_k_cache, L1_cond_v_cache, itok_Bx16_0_63, itok_B_207_1644)
    return x

_drawn_inputs = setup_inputs


def setup_inputs(seed=0):
    import zlib

    import numpy as np

    out = dict(_drawn_inputs(seed))
    spreads = {}
    factors = {'L0_cond_Wr': 5.345,
     'L1_cond_Wk': 23.72,
     'L1_cond_Wv': 32.996,
     'L1_cond_q_norm_w': 4.061,
     'L1_cond_k_norm_w': 8.0,
     'L1_cond_k_cache': 8.0,
     'L1_cond_v_cache': 8.0}
    for name, (base, spread) in spreads.items():
        noise = np.random.default_rng([zlib.crc32(name.encode()), seed]).standard_normal(out[name].shape)
        drawn = base * np.exp(spread * noise) if base else spread * noise
        out[name] = jnp.asarray(drawn.astype(out[name].dtype))
    for name, factor in factors.items():
        out[name] = (out[name] * factor).astype(out[name].dtype)
    return out
```

```python
import math
from contextlib import ExitStack

import concourse.bass as bass
import numpy as np
from concourse import mybir

FP32 = mybir.dt.float32
FP32R = mybir.dt.float32r
I32 = mybir.dt.int32
U32 = mybir.dt.uint32
ALU = mybir.AluOpType
ACT = mybir.ActivationFunctionType
AX = mybir.AxisListType

P = 128
ROWS, DM = 8, 512
KT = DM // P
EXPERTS, RANK = 8, 16
ER = EXPERTS * RANK
HD = 128
KVH, REP = 8, 4
QW = REP * HD
PAGE, NPP = 32, 16
CACHE = PAGE * NPP
KEYS = CACHE + P
TILES = KEYS // P
CT = CACHE // P
GROUPS = KVH * ROWS
TURNS = GROUPS // 2
PAIRS = ROWS // 2
UNITS = REP * TILES // 4
CTX = 4 * HD + 32
HL = ER + EXPERTS
EPS = 1e-6
NEG = -1e30
LANG_BIAS = 5.0
LORA_SCALE = 2.0
TWO_PI = 2 * math.pi
ROUND = 1.5 * 2.0 ** 23


def two_pi_parts():
    a = round(TWO_PI * 64) / 64
    b = round((TWO_PI - a) * 2 ** 17) / 2 ** 17
    return a, b, TWO_PI - a - b


def build(nc, x, lang, table, lens, w0, wr, la, lb, wq, wk, wv, wo, qn, kn, kc, vc, invf, out):
    ctx = ExitStack()
    with ctx:
        def sb(name, shape, dt=FP32):
            return ctx.enter_context(nc.sbuf_tensor(name, shape, dt))

        def ps(name, shape):
            return ctx.enter_context(nc.psum_tensor(name, shape, FP32))

        def sem(name):
            return ctx.enter_context(nc.semaphore(name))

        wqT = sb("wqT", [P, 2, 2, KT, QW], FP32R)
        wkvT = sb("wkvT", [P, 2, 2, KT, 2 * HD], FP32R)
        woT = sb("woT", [P, 2, 2, REP, DM], FP32R)
        xs = sb("xs", [P, 2, 2, KT, P], FP32R)
        rope = sb("rope", [P, 2, CTX])
        kraw = sb("kraw", [P, 2, CT, HD])
        vraw = sb("vraw", [P, 2, CT, HD])
        kT = sb("kT", [P, 2, 2, KEYS], FP32R)
        vs = sb("vs", [P, 2, 2, TILES, HD], FP32R)
        qT = sb("qT", [P, 2, 2, REP, P], FP32R)
        pr = sb("pr", [P, REP, KEYS])
        pt = sb("pt", [P, 2, REP, TILES, P], FP32R)
        ot = sb("ot", [P, 2, REP, P], FP32R)
        mask = sb("mask", [P, 2, KEYS])
        qwork = sb("qwork", [P, 5, QW])
        kwork = sb("kwork", [P, 6, HD])
        wraw = sb("wraw", [P, 2, QW + 2 * HD])
        acc = sb("acc", [P, ROWS, DM])
        ident = sb("ident", [P, P])
        keyno = sb("keyno", [P, CACHE])
        pageidx = sb("pageidx", [P, ROWS, CT])
        kidx = sb("kidx", [P, 2, CT], U32)
        tab = sb("tab", [P, ROWS * NPP], I32)
        small = sb("small", [P, 128])
        qs, sq, u1, u2, qr = (qwork[:, i, :] for i in range(5))
        ks = kwork[:, 0:2, :].rearrange("p a n -> p (a n)")
        kr1, kr2, kr, ksq = (kwork[:, i, :] for i in range(2, 6))
        maxs, nbias, sums, rinv = (small[:, 4 * i:4 * i + 4] for i in range(4))
        ssq = small[:, 16:24].rearrange("p (j h) -> p j h", j=2)
        rq = small[:, 24:32].rearrange("p (j h) -> p j h", j=2)
        ssk, rk, half = small[:, 32:33], small[:, 33:34], small[:, 36:40]
        ssk1 = small[:, 34:35]
        one4 = small[:, 40:44]
        tok8 = small[:, 44:45]
        tokf = small[:, 45:46]
        lenf = small[:, 48:56]
        langf = small[:, 56:64]
        ints = small[:, 64:80].bitcast(I32)
        posf = small[:, 80:88]
        m1, m2, top1, p1, p2 = (small[:, 88 + 8 * i:96 + 8 * i] for i in range(5))
        w0T = wqT[:, 1]
        raT = wkvT[:, 1].rearrange("p a t n -> p (a t n)")[:, 0:2 * KT * HL].rearrange(
            "p (a t n) -> p a t n", a=2, t=KT)
        lbT = woT[:, 1, :, 0, :]
        hgT = woT[:, 1, :, 1, 0:2 * P].rearrange("p a (j n) -> p j a n", j=2)
        x0 = mask
        hl = rope[:, :, :].rearrange("p j n -> p (j n)")[:, 0:ROWS * HL].rearrange("p (b n) -> p b n", b=ROWS)
        gwork = kwork[:, :, :].rearrange("p a n -> p (a n)").rearrange("p (a n) -> p a n", n=ROWS * EXPERTS)
        hg = [ot[:, 0, 0, :], ot[:, 0, 1, :]]
        x1 = [qwork[:, 3, :], qwork[:, 4, :]]
        ang, turns, sint, cost = (qwork[:, i, :] for i in range(4))
        comp = [pr[:, 2 * i:2 * i + 2, :].rearrange("p a n -> p (a n)")[:, 0:ROWS * HD].rearrange(
            "p (b n) -> p b n", b=ROWS) for i in range(2)]
        wn = keyno[:, :].rearrange("p (a n) -> p a n", a=4)
        hgb = sb("hgb", [P, 2, P])

        xT_d = nc.dram_tensor("xT_scratch", (ROWS, P, 2 * KT * P), FP32, kind="Internal").ap()
        rope_d = nc.dram_tensor("rope_scratch", (ROWS, P, CTX), FP32, kind="Internal").ap()

        bS = ps("bS", [P, 1024])[:, 0:KEYS]
        bT = [ps("bT0", [P, 512]), ps("bT1", [P, 512])]
        bQ, bK, bO, bW = (ps(n, [P, 512]) for n in ("bQ", "bK", "bO", "bW"))

        scores_done, kc_done, q_done, kv_done = (sem(n) for n in ("scores_done", "kc_done", "q_done", "kv_done"))
        qT_done, kT_done, pT_done, pv_done, wo_done = (
            sem(n) for n in ("qT_done", "kT_done", "pT_done", "pv_done", "wo_done"))
        wqT_done, woT_done = sem("wqT_done"), sem("woT_done")
        kc_hi, kc_lo, kn_hi, kn_lo, qT_hi, qT_lo = (
            sem(n) for n in ("kc_hi", "kc_lo", "kn_hi", "kn_lo", "qT_hi", "qT_lo"))
        p_hi, p_lo, o_hi, o_lo = (sem(n) for n in ("p_hi", "p_lo", "o_hi", "o_lo"))
        wq_hi, wq_lo, wkv_hi, wkv_lo, wo_hi, wo_lo = (
            sem(n) for n in ("wq_hi", "wq_lo", "wkv_hi", "wkv_lo", "wo_hi", "wo_lo"))
        q_copied, q_squared, q_summed, rq_ready, qr_ready = (
            sem(n) for n in ("q_copied", "q_squared", "q_summed", "rq_ready", "qr_ready"))
        kv_copied, k_squared, rk_ready, kr_ready = (
            sem(n) for n in ("kv_copied", "k_squared", "rk_ready", "kr_ready"))
        max_done, bias_ready, exp_done, rinv_ready, norm_even, norm_odd = (
            sem(n) for n in ("max_done", "bias_ready", "exp_done", "rinv_ready", "norm_even", "norm_odd"))
        mask_ready, vc_split, vn_split, added = (sem(n) for n in ("mask_ready", "vc_split", "vn_split", "added"))
        x_in, rope_in, k_in, v_in, w_in = ([sem(f"{n}{j}") for j in range(2)] for n in
                                           ("x_in", "rope_in", "k_in", "v_in", "w_in"))
        held = sem("held")
        dve_step, pool_step, act_step = sem("dve_step"), sem("pool_step"), sem("act_step")
        rq_arg, rk_arg, q_mul, k_mul, vc_hi, vn_hi = (
            sem(n) for n in ("rq_arg", "rk_arg", "q_mul", "k_mul", "vc_hi", "vn_hi"))
        lens_ready = sem("lens_ready")
        consts_in, ident_ready, const_ready = sem("consts_in"), sem("ident_ready"), sem("const_ready")
        idx_step = sem("idx_step")
        prep_in = [sem(f"prep_in{i}") for i in range(6)]
        prep_T, prep_hi, prep_lo = sem("prep_T"), sem("prep_hi"), sem("prep_lo")
        acc_in, tile_in = sem("acc_in"), [sem("tile_in0"), sem("tile_in1")]
        a_T, a_hi, a_lo, a_proj, a_hl, a_add = (sem(n) for n in ("a_T", "a_hi", "a_lo", "a_proj", "a_hl", "a_add"))
        experts_ready, diff_ready, wn_ready = sem("experts_ready"), sem("diff_ready"), sem("wn_ready")
        c_hg, c_T, c_hi, c_lo, c_lora, c_x1, c_acc, c_xT, c_xhi, c_xlo = (
            sem(n) for n in ("c_hg", "c_T", "c_hi", "c_lo", "c_lora", "c_x1", "c_acc", "c_xT", "c_xhi", "c_xlo"))
        c_out = [sem("c_out0"), sem("c_out1")]
        angle_ready, sin_ready, cosarg_ready, cos_ready = (
            sem(n) for n in ("angle_ready", "sin_ready", "cosarg_ready", "cos_ready"))
        comp_ready, comp_out, lens_out = sem("comp_ready"), [sem("comp_out0"), sem("comp_out1")], sem("lens_out")
        out_stored = sem("out_stored")

        def wait(eng, s, n):
            if not isinstance(n, int) or n > 0:
                eng.wait_ge(s, n)

        def hold(eng):
            eng.sem_inc(held, 1)

        prep = []
        for ot_ in range(KT):
            prep.append((w0[ot_ * P:(ot_ + 1) * P, :], P, [w0T[:, a, :, ot_ * P:(ot_ + 1) * P] for a in range(2)]))
        prep.append((la.rearrange("e r d -> (e r) d"), P, [raT[:, a, :, 0:ER] for a in range(2)]))
        prep.append((wr, EXPERTS, [raT[:, a, :, ER:HL] for a in range(2)]))
        prep.append((None, P, [lbT[:, a, :].rearrange("p (t n) -> p t n", t=KT) for a in range(2)]))
        for e in range(REP):
            prep.append((wq[e * P:(e + 1) * P, :], P, [wqT[:, 0, a, :, e * P:(e + 1) * P] for a in range(2)]))
        prep.append((wk[0:HD, :], P, [wkvT[:, 0, a, :, 0:HD] for a in range(2)]))
        prep.append((wv[0:HD, :], P, [wkvT[:, 0, a, :, HD:2 * HD] for a in range(2)]))
        for o in range(KT):
            prep.append((wo[o * P:(o + 1) * P, 0:QW], P, [woT[:, 0, a, :, o * P:(o + 1) * P] for a in range(2)]))
        NPREP = len(prep)
        loads = [EXPERTS if w[0] is None else 1 for w in prep]
        prep_count = [16 * sum(loads[i % 6:i + 1:6]) for i in range(NPREP)]
        N0 = 7
        stage = [kraw[:, 0].rearrange("p t n -> p (t n)"), kraw[:, 1].rearrange("p t n -> p (t n)"),
                 vraw[:, 0].rearrange("p t n -> p (t n)"), vraw[:, 1].rearrange("p t n -> p (t n)"),
                 wraw[:, 0, 0:QW], wraw[:, 1, 0:QW]]
        prep_bank = [bW, bK]

        def at(i, n=1):
            return slice(i * n, (i + 1) * n) if isinstance(i, int) else bass.ds(i * n, n)

        def part_of(view, kv, a, tile):
            return view[:, at(kv % 2), a, tile, :].rearrange("p k n -> p (k n)")

        def columns_of(view, t, a):
            return view[:, at((t // PAIRS + 1) % 2), a, :, at(t % PAIRS, P)].rearrange("p k t n -> p (k t) n")

        def tile_of(view, t, a):
            return view[:, at((t // PAIRS + 1) % 2), a, at(t % PAIRS), :].rearrange("p k t n -> p (k t n)")

        def kv_of_next(t, j):
            return t // PAIRS if j == 0 else (t + 1) // PAIRS

        def kv_of_last(t, j):
            return (t - 1) // PAIRS if j == 0 else t // PAIRS

        block = ctx.enter_context(nc.Block())

        @block.sync
        def _(sp):
            sp.dma_start(tab[:, :], table.rearrange("b n -> (b n)").partition_broadcast(P)).then_inc(consts_in, 16)
            sp.dma_start(ints[:, 0:8], lens.partition_broadcast(P)).then_inc(consts_in, 16)
            sp.dma_start(ints[:, 8:16], lang.partition_broadcast(P)).then_inc(consts_in, 16)
            sp.dma_start(wn[:, 0, :], qn.partition_broadcast(P)).then_inc(consts_in, 16)
            sp.dma_start(wn[:, 2, :], kn.partition_broadcast(P)).then_inc(consts_in, 16)
            sp.dma_start(wn[:, 1, 0:HD // 2], invf.partition_broadcast(P)).then_inc(consts_in, 16)

            def load_weight(i):
                src, n, _ = prep[i]
                if i >= 6:
                    sp.wait_ge(prep_T, i - 5)
                dst = stage[i % 6]
                if src is None:
                    for e in range(EXPERTS):
                        d = dst.rearrange("p (t e r) -> p t e r", t=KT, e=EXPERTS)[:, :, e, :]
                        sp.dma_start(d, lb[e].rearrange("(t p) r -> p t r", p=P)).then_inc(prep_in[i % 6], 16)
                else:
                    sp.dma_start(dst[0:n, :], src).then_inc(prep_in[i % 6], 16)

            def load_tile(b, j, k):
                wait(sp, a_T, b - 1)
                sp.dma_start(x0[:, j, 0:DM], x[at(b)].rearrange("a p n -> p (a n)")).then_inc(tile_in[j], 16)

            load_tile(0, 0, 0)
            load_tile(1, 1, 0)
            for i in range(6):
                load_weight(i)
            sp.dma_start(acc[:, :, :], x.rearrange("b p n -> p b n")).then_inc(acc_in, 16)
            for i in range(6, N0):
                load_weight(i)
            for b in range(2, ROWS):
                load_tile(b, b % 2, b // 2)
                load_weight(N0 + b - 2)
            for i in range(N0 + ROWS - 2, NPREP):
                load_weight(i)

            for i in range(4):
                sp.wait_ge(comp_ready, i + 1)
                sp.dma_start(rope_d[:, :, i * HD:(i + 1) * HD].rearrange("b p n -> p b n"),
                             comp[i % 2]).then_inc(comp_out[i % 2], 16)
            sp.wait_ge(lens_ready, 1)
            sp.dma_start(rope_d[:, :, 4 * HD:4 * HD + 1].rearrange("b p n -> p b n"),
                         lenf.unsqueeze(2), allow_slow_non_contiguous=True).then_inc(lens_out, 16)
            with sp.Fori(0, PAIRS) as u:
                for j in range(2):
                    sp.wait_ge(c_xlo, 2 * u + j + 1)
                    sp.dma_start(xT_d[bass.ds(2 * u + j, 1)].rearrange("a p n -> p (a n)"),
                                 xs[:, j].rearrange("p a t n -> p (a t n)").bitcast(FP32)).then_inc(c_out[j], 16)
            sp.wait_ge(c_out[0], 16 * PAIRS)
            sp.wait_ge(c_out[1], 16 * PAIRS)
            sp.wait_ge(comp_out[0], 32)
            sp.wait_ge(comp_out[1], 32)
            sp.wait_ge(lens_out, 16)
            sp.wait_ge(prep_T, NPREP)

            def load_group(b, j):
                sp.dma_start(xs[:, j].rearrange("p a t n -> p (a t n)").bitcast(FP32),
                             xT_d[at(b)].rearrange("a p n -> p (a n)")).then_inc(x_in[j], 16)
                sp.dma_start(rope[:, j, 0:4 * HD + 1],
                             rope_d[at(b), :, 0:4 * HD + 1].rearrange("a p n -> p (a n)")).then_inc(rope_in[j], 16)

            def load_weights(j, kv, part):
                if j == 0:
                    sp.dma_start(wraw[:, 0, 0:QW], wq[at(kv * REP + part, P), :]).then_inc(w_in[0], 16)
                    sp.dma_start(wraw[:, 0, QW:QW + HD], wk[at(kv, HD), at(part, P)]).then_inc(w_in[0], 16)
                    sp.dma_start(wraw[:, 0, QW + HD:QW + 2 * HD], wv[at(kv, HD), at(part, P)]).then_inc(w_in[0], 16)
                else:
                    sp.dma_start(wraw[:, 1, 0:QW], wo[at(part, P), at(kv, QW)]).then_inc(w_in[1], 16)

            def turn(t, store):
                for j in range(2):
                    g = 2 * t + j
                    wait(sp, kv_done, g + 1)
                    wait(sp, qr_ready, g + 1)
                    wait(sp, kr_ready, g + 1)
                    wait(sp, mask_ready, g + 1)
                    load_group(((t + 1) % PAIRS) * 2 + j, j)
                    u = t if j == 0 else t + 1
                    if j == 0:
                        wait(sp, woT_done, t)
                        load_weights(1, (u // PAIRS + 1) % KVH, u % PAIRS)
                    else:
                        wait(sp, wqT_done, t + 1)
                        wait(sp, kT_done, 2 * t + 2)
                        load_weights(0, (u // PAIRS + 1) % KVH, u % PAIRS)
                    if store:
                        store_row(g - 2)

            def store_row(g):
                sp.wait_ge(added, g + 1)
                b = g % ROWS
                sp.dma_start(out[at(b)].rearrange("a p n -> p (a n)"),
                             acc[:, at(b), :].rearrange("p a n -> p (a n)")).then_inc(out_stored, 16)

            load_group(0, 0)
            load_group(1, 1)
            load_weights(0, 1, 0)
            turn(0, False)
            with sp.Fori(1, TURNS - 3) as t:
                turn(t, False)
            with sp.Fori(TURNS - 3, TURNS - 1) as t:
                turn(t, True)
            for g in range(GROUPS - 4, GROUPS):
                store_row(g)
            sp.wait_ge(out_stored, 16 * ROWS)

        @block.tensor
        def _(pe):
            def mm3(dst, lhs, rhs, first, last):
                nc.tensor.matmul(dst, lhs[0], rhs[0], start=first, stop=False)
                nc.tensor.matmul(dst, lhs[0], rhs[1], start=False, stop=False)
                return nc.tensor.matmul(dst, lhs[1], rhs[0], start=False, stop=last)

            pe.wait_ge(ident_ready, 1)

            def prep_unit(i):
                _, n, _ = prep[i]
                pe.wait_ge(prep_in[i % 6], prep_count[i])
                if i >= 2:
                    pe.wait_ge(prep_lo, i - 1)
                bank = prep_bank[i % 2]
                for c in range(KT):
                    src = stage[i % 6][0:n, c * P:(c + 1) * P]
                    last = nc.tensor.transpose(bank[:, c * n:(c + 1) * n], src, ident[0:n, 0:n])
                last.then_inc(prep_T, 1)

            for i in range(N0):
                prep_unit(i)

            with pe.Fori(0, PAIRS) as u:
                for j in range(2):
                    pe.wait_ge(tile_in[j], 16 * u + 16)
                    if j == 0:
                        pe.wait_ge(prep_lo, N0)
                    for c in range(KT):
                        last = nc.tensor.transpose(prep_bank[j][:, c * P:(c + 1) * P], x0[:, j, c * P:(c + 1) * P],
                                                   ident[:, :])
                    last.then_inc(a_T, 1)
                for j in range(2):
                    b = 2 * u + j
                    pe.wait_ge(a_lo, b + 1)
                    for c in range(KT):
                        mm3(bT[j][:, :], [xs[:, j, a, c, :] for a in range(2)],
                            [w0T[:, a, c, :] for a in range(2)], c == 0, c == KT - 1)
                    for c in range(KT):
                        last = mm3([bQ, bO][j][:, 0:HL], [xs[:, j, a, c, :] for a in range(2)],
                                   [raT[:, a, c, :] for a in range(2)], c == 0, c == KT - 1)
                    last.then_inc(a_proj, 1)
                pe.wait_ge(a_add, 2 * u + 2)
                pe.wait_ge(a_hl, 2 * u + 2)

            for i in range(N0, NPREP):
                prep_unit(i)
            pe.wait_ge(prep_lo, NPREP)
            with pe.Fori(0, PAIRS) as u:
                for j in range(2):
                    pe.wait_ge(c_hg, 2 * u + j + 1)
                    nc.tensor.transpose(prep_bank[j][:, 0:P], hgb[:, j, :], ident[:, :]).then_inc(c_T, 1)
                for j in range(2):
                    pe.wait_ge(c_lo, 2 * u + j + 1)
                    mm3(bT[j][:, :], [hgT[:, j, a, :] for a in range(2)], [lbT[:, a, :] for a in range(2)],
                        True, True).then_inc(c_lora, 1)
                for j in range(2):
                    pe.wait_ge(c_x1, 2 * u + j + 1)
                    for c in range(KT):
                        last = nc.tensor.transpose([bQ, bO][j][:, c * P:(c + 1) * P], x1[j][:, c * P:(c + 1) * P],
                                                   ident[:, :])
                    last.then_inc(c_xT, 1)
                pe.wait_ge(c_xlo, 2 * u + 2)

            def scores(t, j, h):
                g = 2 * t + j
                if h == 0:
                    pe.wait_ge(kc_lo, g + 1)
                    pe.wait_ge(kn_lo, g + 1)
                    pe.wait_ge(qT_lo, g + 1)
                wait(pe, max_done, 4 * g + h)
                qh = [qT[:, j, a, h, :] for a in range(2)]
                mm3(bS[:, 0:CACHE], qh, [kT[:, j, a, 0:CACHE] for a in range(2)], True, True)
                mm3(bS[:, CACHE:KEYS], qh, [kT[:, j, a, CACHE:KEYS] for a in range(2)],
                    True, True).then_inc(scores_done, 1)

            def k_cache_T(t, j):
                n, m, uses = 2 * t + j + 1, (j + 1) % 2, t + 1 + j
                wait(pe, vn_hi, n)
                pe.wait_ge(k_in[m], 64 * uses)
                for c in range(CT):
                    last = nc.tensor.transpose(bK[:, c * P:(c + 1) * P], kraw[:, m, c, :], ident[:, :])
                last.then_inc(kc_done, 1)

            def q_proj(t, j):
                n, m, uses, kv = 2 * t + j + 1, (j + 1) % 2, t + 1 + j, kv_of_next(t, j)
                wait(pe, kn_lo, n)
                pe.wait_ge(x_in[m], 16 * uses)
                if j == 1:
                    wait(pe, wkv_lo, t + 1)
                    wait(pe, wq_lo, t + 1)
                for c in range(KT):
                    last = mm3(bQ[:, :], [xs[:, m, a, c, :] for a in range(2)],
                               [part_of(wqT, kv, a, c) for a in range(2)], c == 0, c == KT - 1)
                last.then_inc(q_done, 1)

            def kv_proj(t, j):
                n, m, kv = 2 * t + j + 1, (j + 1) % 2, kv_of_next(t, j)
                pe.wait_ge(kc_lo, n + 1)
                for c in range(KT):
                    last = mm3(bK[:, 0:2 * HD], [xs[:, m, a, c, :] for a in range(2)],
                               [part_of(wkvT, kv, a, c) for a in range(2)], c == 0, c == KT - 1)
                last.then_inc(kv_done, 1)

            def q_T(t, j):
                n = 2 * t + j + 1
                pe.wait_ge(qr_ready, n + 1)
                wait(pe, wq_lo if j else wo_lo, t + 1 if j else t)
                for h in range(REP):
                    last = nc.tensor.transpose(bW[:, h * P:(h + 1) * P], qr[:, h * P:(h + 1) * P], ident[:, :])
                last.then_inc(qT_done, 1)

            def k_new_T(t, j, weights):
                n = 2 * t + j + 1
                pe.wait_ge(kr_ready, n + 1)
                pe.wait_ge(q_copied, n + 1)
                last = nc.tensor.transpose(bQ[:, 0:P], kr, ident[:, :])
                if weights:
                    pe.wait_ge(w_in[0], 48 * (t + 1))
                    for i in range(2):
                        last = nc.tensor.transpose(bQ[:, (1 + i) * P:(2 + i) * P],
                                                   wraw[:, 0, QW + i * P:QW + (i + 1) * P], ident[:, :])
                last.then_inc(kT_done, 1)

            def w_T(t, j):
                pe.wait_ge(w_in[j], (48 if j == 0 else 16) * (t + 1))
                pe.wait_ge(qT_lo, 2 * t + j + 2)
                for c in range(4):
                    last = nc.tensor.transpose(bW[:, c * P:(c + 1) * P], wraw[:, j, c * P:(c + 1) * P], ident[:, :])
                last.then_inc(woT_done if j else wqT_done, 1)

            def probs_T(t, j, k):
                g = 2 * t + j
                wait(pe, p_lo, UNITS * g + k - 1)
                h = min(REP - 1, (4 * k + 3) // TILES)
                if h % 2 == 0 or k == UNITS - 1:
                    pe.wait_ge(norm_even, 2 * g + (h // 2) + 1)
                if h % 2 == 1:
                    pe.wait_ge(norm_odd, 2 * g + h // 2 + 1)
                for i in range(4):
                    tile = 4 * k + i
                    last = nc.tensor.transpose(bT[(j + k) % 2][:, i * P:(i + 1) * P],
                                               pr[:, tile // TILES, (tile % TILES) * P:(tile % TILES + 1) * P],
                                               ident[:, :])
                last.then_inc(pT_done, 1)

            def values(t, j):
                f, m = 2 * t + j - 1, (j + 1) % 2
                wait(pe, added, f)
                pe.wait_ge(p_lo, UNITS * f + UNITS)
                pe.wait_ge(vn_split, f + 1)
                pe.wait_ge(vc_split, f + 1)
                for c in range(TILES):
                    last = mm3(bO[:, :], [vs[:, m, a, c, :] for a in range(2)],
                               [pt[:, a, :, c, :] for a in range(2)], c == 0, c == TILES - 1)
                last.then_inc(pv_done, 1)

            def out_proj(t, j):
                f, kv = 2 * t + j - 1, kv_of_last(t, j)
                pe.wait_ge(o_lo, f + 1)
                for h in range(REP):
                    last = mm3(bO[:, :], [ot[:, a, h, :] for a in range(2)],
                               [part_of(woT, kv, a, h) for a in range(2)], h == 0, h == REP - 1)
                last.then_inc(wo_done, 1)

            def turn(t, first=False, last=False):
                for j in range(2):
                    prev, nxt, weights = not (first and j == 0), not (last and j == 1), not last
                    scores(t, j, 0)
                    if nxt:
                        k_cache_T(t, j)
                        q_proj(t, j)
                    scores(t, j, 1)
                    if prev:
                        values(t, j)
                    scores(t, j, 2)
                    probs_T(t, j, 0)
                    if nxt:
                        kv_proj(t, j)
                    scores(t, j, 3)
                    probs_T(t, j, 1)
                    if nxt:
                        q_T(t, j)
                    if prev:
                        out_proj(t, j)
                    if nxt:
                        k_new_T(t, j, j == 0 and weights)
                    probs_T(t, j, 2)
                    if weights:
                        w_T(t, j)
                    probs_T(t, j, 3)
                    probs_T(t, j, 4)

            k_cache_T(-1, 1)
            q_proj(-1, 1)
            kv_proj(-1, 1)
            q_T(-1, 1)
            k_new_T(-1, 1, False)
            turn(0, first=True)
            with pe.Fori(1, TURNS - 1) as t:
                turn(t)
            turn(TURNS - 1, last=True)
            values(TURNS, 0)
            out_proj(TURNS, 0)

        @block.scalar
        def _(act):
            def take(dst, src):
                return nc.scalar.activation(dst, src, ACT.Copy)

            def prep_take(i):
                _, n, dst = prep[i]
                act.wait_ge(prep_T, i + 1)
                take(dst[0], prep_bank[i % 2][:, 0:KT * n].rearrange("p (t n) -> p t n", t=KT)).then_inc(prep_hi, 1)

            for i in range(N0):
                prep_take(i)
            with act.Fori(0, PAIRS) as u:
                for j in range(2):
                    act.wait_ge(a_T, 2 * u + j + 1)
                    take(xs[:, j, 0].rearrange("p t n -> p (t n)"), prep_bank[j][:, :]).then_inc(a_hi, 1)
                for j in range(2):
                    b = 2 * u + j
                    act.wait_ge(a_proj, b + 1)
                    hold(act)
                    take(hl[:, bass.ds(b, 1), :], [bQ, bO][j][:, 0:HL].unsqueeze(1)).then_inc(a_hl, 1)
            act.wait_ge(angle_ready, 1)
            nc.scalar.activation(sint, ang, ACT.Sin).then_inc(sin_ready, 1)
            act.wait_ge(cosarg_ready, 1)
            nc.scalar.activation(cost, turns, ACT.Sin).then_inc(cos_ready, 1)
            for i in range(N0, NPREP):
                prep_take(i)
            act.wait_ge(diff_ready, 1)
            nc.scalar.activation(p2, m2, ACT.Exp).then_inc(act_step, 1)
            with act.Fori(0, PAIRS) as u:
                for j in range(2):
                    act.wait_ge(c_T, 2 * u + j + 1)
                    take(hgT[:, j, 0, :], prep_bank[j][:, 0:P]).then_inc(c_hi, 1)
                for j in range(2):
                    act.wait_ge(c_xT, 2 * u + j + 1)
                    take(xs[:, j, 0].rearrange("p t n -> p (t n)"), [bQ, bO][j][:, :]).then_inc(c_xhi, 1)
                for j in range(2):
                    act.wait_ge(c_out[j], 16 * u + 16)

            def k_cache_hi(t, j):
                n, m = 2 * t + j + 1, (j + 1) % 2
                act.wait_ge(kc_done, n + 1)
                take(kT[:, m, 0, 0:CACHE], bK[:, :]).then_inc(kc_hi, 1)

            def values_cache_hi(t, j):
                n, m, uses = 2 * t + j + 1, (j + 1) % 2, t + 1 + j
                act.wait_ge(v_in[m], 16 * CT * uses)
                wait(act, pv_done, n - 1)
                take(vs[:, m, 0, 0:CT, :], vraw[:, m]).then_inc(vc_hi, 1)

            def q_out(t, j):
                n, m = 2 * t + j + 1, (j + 1) % 2
                act.wait_ge(q_done, n + 1)
                wait(act, qr_ready, n)
                take(qs, bQ[:, :]).then_inc(q_copied, 1)
                act.wait_ge(q_copied, n + 1)
                wait(act, q_summed, n)
                nc.scalar.activation(sq, qs, ACT.Square).then_inc(q_squared, 1)

            def kv_out(t, j):
                n, m = 2 * t + j + 1, (j + 1) % 2
                act.wait_ge(kv_done, n + 1)
                wait(act, kr_ready, n)
                wait(act, vn_split, n)
                take(ks, bK[:, 0:2 * HD]).then_inc(kv_copied, 1)
                take(vs[:, m, 0, CT, :], bK[:, HD:2 * HD]).then_inc(vn_hi, 1)
                act.wait_ge(kv_copied, n + 1)
                wait(act, rk_ready, n)
                nc.scalar.activation(ksq, ks[:, 0:HD], ACT.Square, accum_out=ssk).then_inc(k_squared, 1)

            def exps(t, j, h):
                g = 2 * t + j
                act.wait_ge(bias_ready, 4 * g + h + 1)
                nc.scalar.activation(pr[:, h, :], pr[:, h, :], ACT.Exp, bias=nbias[:, h:h + 1],
                                     scale=rq[:, j, h:h + 1], accum_out=sums[:, h:h + 1]).then_inc(exp_done, 1)

            def normalise(t, j, h):
                g = 2 * t + j
                act.wait_ge(rinv_ready, 4 * g + h + 1)
                nc.scalar.activation(pr[:, h, :], pr[:, h, :], ACT.Copy,
                                     scale=rinv[:, h:h + 1]).then_inc(norm_odd, 1)

            def o_hi_out(t, j):
                act.wait_ge(pv_done, 2 * t + j)
                take(ot[:, 0].rearrange("p h n -> p (h n)"), bO[:, :]).then_inc(o_hi, 1)

            def probs_hi(t, j, k):
                g = 2 * t + j
                act.wait_ge(pT_done, UNITS * g + k + 1)
                take(pt[:, 0].rearrange("p h t n -> p (h t n)")[:, k * 512:(k + 1) * 512],
                     bT[(j + k) % 2][:, :]).then_inc(p_hi, 1)

            def q_T_hi(t, j):
                n, m = 2 * t + j + 1, (j + 1) % 2
                act.wait_ge(qT_done, n + 1)
                take(qT[:, m, 0].rearrange("p h n -> p (h n)"), bW[:, :]).then_inc(qT_hi, 1)

            def k_new_hi(t, j):
                n, m = 2 * t + j + 1, (j + 1) % 2
                act.wait_ge(kT_done, n + 1)
                take(kT[:, m, 0, CACHE:KEYS], bQ[:, 0:P]).then_inc(kn_hi, 1)

            def wkv_take(t):
                act.wait_ge(kT_done, 2 * t + 2)
                hold(act)
                take(tile_of(wkvT, t, 0), bQ[:, P:3 * P]).then_inc(wkv_hi, 1)

            def w_take(t, j):
                act.wait_ge(woT_done if j else wqT_done, t + 1)
                hold(act)
                take(columns_of(woT if j else wqT, t, 0), bW[:, :].rearrange("p (c n) -> p c n", c=4)).then_inc(
                    wo_hi if j else wq_hi, 1)

            def turn(t, first=False, last=False):
                for j in range(2):
                    prev, nxt, weights = not (first and j == 0), not (last and j == 1), not last
                    if nxt:
                        k_cache_hi(t, j)
                    exps(t, j, 0)
                    if nxt:
                        q_out(t, j)
                    exps(t, j, 1)
                    normalise(t, j, 1)
                    if nxt:
                        values_cache_hi(t, j)
                    if prev:
                        o_hi_out(t, j)
                    probs_hi(t, j, 0)
                    exps(t, j, 2)
                    if nxt:
                        kv_out(t, j)
                    probs_hi(t, j, 1)
                    if nxt:
                        q_T_hi(t, j)
                    exps(t, j, 3)
                    normalise(t, j, 3)
                    if nxt:
                        k_new_hi(t, j)
                        if j == 0 and weights:
                            wkv_take(t)
                    probs_hi(t, j, 2)
                    if weights:
                        w_take(t, j)
                    probs_hi(t, j, 3)
                    probs_hi(t, j, 4)

            k_cache_hi(-1, 1)
            values_cache_hi(-1, 1)
            q_out(-1, 1)
            kv_out(-1, 1)
            q_T_hi(-1, 1)
            k_new_hi(-1, 1)
            turn(0, first=True)
            with act.Fori(1, TURNS - 1) as t:
                turn(t)
            turn(TURNS - 1, last=True)
            o_hi_out(TURNS, 0)

        @block.vector
        def _(dve):
            steps = [0]

            def step(ins):
                steps[0] += 1
                ins.then_inc(dve_step, 1)
                dve.wait_ge(dve_step, steps[0])

            def rest(dst, src, hi):
                return nc.vector.tensor_tensor(dst, src, hi.bitcast(FP32), ALU.subtract)

            def prep_rest(i):
                _, n, dst = prep[i]
                dve.wait_ge(prep_hi, i + 1)
                rest(dst[1], prep_bank[i % 2][:, 0:KT * n].rearrange("p (t n) -> p t n", t=KT),
                     dst[0]).then_inc(prep_lo, 1)

            dve.wait_ge(consts_in, 16 * 6)
            dve.wait_ge(const_ready, 1)
            step(nc.vector.tensor_copy(lenf, ints[:, 0:8]))
            nc.vector.tensor_copy(langf, ints[:, 8:16]).then_inc(lens_ready, 1)
            step(nc.vector.tensor_scalar(posf, lenf, tokf, None, ALU.add))
            for q in range(4):
                r = slice(q * PAGE, (q + 1) * PAGE)
                step(nc.vector.tensor_copy(pageidx[r, :, :],
                                           tab[r, :].rearrange("p (b c q) -> p b c q", b=ROWS, q=4)[:, :, :, q]))
                step(nc.vector.tensor_scalar(pageidx[r, :, :], pageidx[r, :, :], 0.0, 63.0, ALU.max, ALU.min))
                step(nc.vector.tensor_scalar(pageidx[r, :, :], pageidx[r, :, :], float(PAGE * KVH),
                                             float(-q * PAGE * KVH), ALU.mult, ALU.add))
            nc.vector.tensor_scalar(pageidx[:, :, :], pageidx[:, :, :], tok8, None, ALU.add).then_inc(idx_step, 1)
            for i in range(N0):
                prep_rest(i)
            half_hd = HD // 2
            for b in range(ROWS):
                last = nc.vector.tensor_scalar(ang[:, b * half_hd:(b + 1) * half_hd], wn[:, 1, 0:half_hd],
                                               posf[:, b:b + 1], None, ALU.mult)
            step(last)
            step(nc.vector.tensor_scalar(turns, ang, 1.0 / TWO_PI, ROUND, ALU.mult, ALU.add))
            step(nc.vector.tensor_scalar(turns, turns, -ROUND, None, ALU.add))
            for c in two_pi_parts():
                step(nc.vector.scalar_tensor_tensor(ang, turns, -c, ang, ALU.mult, ALU.add))
            nc.vector.tensor_scalar(ang, ang, 3.1415925, -3.1415925, ALU.min, ALU.max).then_inc(angle_ready, 1)
            dve.wait_ge(angle_ready, 1)
            step(nc.vector.scalar_tensor_tensor(turns, ang, -1.0, ang, ALU.mult, ALU.max))
            nc.vector.tensor_scalar(turns, turns, -1.0, math.pi / 2, ALU.mult, ALU.add).then_inc(cosarg_ready, 1)
            root = math.sqrt(HD)
            step(nc.vector.tensor_scalar(wn[:, 1, :], wn[:, 0, :], -1.0, None, ALU.mult))
            step(nc.vector.tensor_copy(wn[:, 1, 0:half_hd], wn[:, 0, 0:half_hd]))
            step(nc.vector.tensor_scalar(wn[:, 2, :], wn[:, 2, :], root, None, ALU.mult))
            step(nc.vector.tensor_scalar(wn[:, 3, :], wn[:, 2, :], -1.0, None, ALU.mult))
            nc.vector.tensor_copy(wn[:, 3, 0:half_hd], wn[:, 2, 0:half_hd]).then_inc(wn_ready, 1)

            dve.wait_ge(acc_in, 16)
            with dve.Fori(0, PAIRS) as u:
                for j in range(2):
                    dve.wait_ge(a_hi, 2 * u + j + 1)
                    rest(xs[:, j, 1].rearrange("p t n -> p (t n)"), prep_bank[j][:, :],
                         xs[:, j, 0].rearrange("p t n -> p (t n)")).then_inc(a_lo, 1)
                for j in range(2):
                    row = acc[:, bass.ds(2 * u + j, 1), :]
                    dve.wait_ge(a_proj, 2 * u + j + 1)
                    nc.vector.tensor_tensor(row, bT[j][:, :].unsqueeze(1), row, ALU.add).then_inc(a_add, 1)
            for i in range(N0, NPREP):
                prep_rest(i)

            dve.wait_ge(a_hl, ROWS)
            dve.wait_ge(experts_ready, 1)
            lg, eq, oh1, oh2, rev, num, gates = (gwork[:, i, :] for i in range(7))

            def by_row(v):
                return v.rearrange("p (b e) -> p b e", b=ROWS)

            def wide(v):
                return v.unsqueeze(2).to_broadcast([P, ROWS, EXPERTS])

            def first_largest(onehot, best):
                step(nc.vector.tensor_reduce(best, by_row(lg), AX.X, ALU.max))
                step(nc.vector.tensor_tensor(by_row(eq), by_row(lg), wide(best), ALU.is_equal))
                step(nc.vector.tensor_tensor(eq, eq, rev, ALU.mult))
                step(nc.vector.tensor_reduce(top1, by_row(eq), AX.X, ALU.max))
                step(nc.vector.tensor_tensor(by_row(onehot), by_row(eq), wide(top1), ALU.is_equal))

            step(nc.vector.tensor_tensor(by_row(eq), by_row(num), wide(langf), ALU.is_equal))
            step(nc.vector.scalar_tensor_tensor(by_row(lg), by_row(eq), LANG_BIAS, hl[:, :, ER:HL], ALU.mult, ALU.add))
            first_largest(oh1, m1)
            step(nc.vector.scalar_tensor_tensor(lg, oh1, -3e38, lg, ALU.mult, ALU.add))
            first_largest(oh2, m2)
            nc.vector.tensor_tensor(m2, m2, m1, ALU.subtract).then_inc(diff_ready, 1)
            dve.wait_ge(act_step, 1)
            step(nc.vector.tensor_scalar(p1, p2, 1.0, None, ALU.add))
            step(nc.vector.reciprocal(p1, p1))
            step(nc.vector.tensor_tensor(p2, p2, p1, ALU.mult))
            step(nc.vector.tensor_tensor(by_row(oh1), by_row(oh1), wide(p1), ALU.mult))
            step(nc.vector.tensor_tensor(by_row(oh2), by_row(oh2), wide(p2), ALU.mult))
            step(nc.vector.tensor_tensor(gates, oh1, oh2, ALU.add))
            step(nc.vector.tensor_scalar(gates, gates, LORA_SCALE, None, ALU.mult))
            dve.wait_ge(comp_ready, 4)
            with dve.Fori(0, PAIRS) as u:
                for j in range(2):
                    b = 2 * u + j
                    nc.vector.tensor_tensor(
                        hgb[:, j, :].rearrange("p (e r) -> p e r", e=EXPERTS),
                        hl[:, bass.ds(b, 1), 0:ER].rearrange("p b (e r) -> p (b e) r", e=EXPERTS),
                        gates[:, bass.ds(b * EXPERTS, EXPERTS)].unsqueeze(2).to_broadcast([P, EXPERTS, RANK]),
                        ALU.mult).then_inc(c_hg, 1)
                for j in range(2):
                    dve.wait_ge(c_hi, 2 * u + j + 1)
                    rest(hgT[:, j, 1, :], prep_bank[j][:, 0:P], hgT[:, j, 0, :]).then_inc(c_lo, 1)
                for j in range(2):
                    dve.wait_ge(c_lora, 2 * u + j + 1)
                    row = acc[:, bass.ds(2 * u + j, 1), :].rearrange("p a n -> p (a n)")
                    nc.vector.tensor_tensor(x1[j], bT[j][:, :], row, ALU.add).then_inc(c_x1, 1)
                for j in range(2):
                    dve.wait_ge(c_xhi, 2 * u + j + 1)
                    rest(xs[:, j, 1].rearrange("p t n -> p (t n)"), [bQ, bO][j][:, :],
                         xs[:, j, 0].rearrange("p t n -> p (t n)")).then_inc(c_xlo, 1)
                dve.wait_ge(c_acc, 2 * u + 2)

            def head_max(t, j, h):
                g = 2 * t + j
                dve.wait_ge(scores_done, 4 * g + h + 1)
                if h == 0:
                    dve.wait_ge(mask_ready, g + 1)
                wait(dve, pT_done, UNITS * (g - 1) + h + 2)
                hold(dve)
                nc.vector.tensor_tensor_reduce(out=pr[:, h, :], in0=bS, in1=mask[:, j, :], scale=1.0, scalar=-3e38,
                                               op0=ALU.add, op1=ALU.max,
                                               accum_out=maxs[:, h:h + 1]).then_inc(max_done, 1)
                dve.wait_ge(max_done, 4 * g + h + 1)
                dve.wait_ge(rq_ready, g + 1)
                nc.vector.scalar_tensor_tensor(nbias[:, h:h + 1], maxs[:, h:h + 1], -1.0, rq[:, j, h:h + 1],
                                               ALU.mult, ALU.mult).then_inc(bias_ready, 1)

            def head_sum(t, j, h):
                g = 2 * t + j
                dve.wait_ge(exp_done, 4 * g + h + 1)
                nc.vector.reciprocal(rinv[:, h:h + 1], sums[:, h:h + 1]).then_inc(rinv_ready, 1)
                if h % 2 == 0:
                    dve.wait_ge(rinv_ready, 4 * g + h + 1)
                    nc.vector.tensor_scalar(pr[:, h, :], pr[:, h, :], rinv[:, h:h + 1], None,
                                            ALU.mult).then_inc(norm_even, 1)

            def k_cache_lo(t, j):
                n, m = 2 * t + j + 1, (j + 1) % 2
                dve.wait_ge(kc_hi, n + 1)
                rest(kT[:, m, 1, 0:CACHE], bK[:, :], kT[:, m, 0, 0:CACHE]).then_inc(kc_lo, 1)

            def make_mask(t, j):
                n, m, uses = 2 * t + j + 1, (j + 1) % 2, t + 1 + j
                dve.wait_ge(rope_in[m], 16 * uses)
                nc.vector.tensor_scalar(mask[:, m, 0:CACHE], keyno[:, :], rope[:, m, 4 * HD:4 * HD + 1], NEG,
                                        ALU.is_ge, ALU.mult).then_inc(mask_ready, 1)

            def values_cache_lo(t, j):
                n, m = 2 * t + j + 1, (j + 1) % 2
                dve.wait_ge(vc_hi, n + 1)
                rest(vs[:, m, 1, 0:CT, :], vraw[:, m], vs[:, m, 0, 0:CT, :]).then_inc(vc_split, 1)

            def q_sum(t, j):
                n, m = 2 * t + j + 1, (j + 1) % 2
                dve.wait_ge(q_squared, n + 1)
                nc.vector.tensor_reduce(ssq[:, m, :], sq.rearrange("p (h n) -> p h n", h=REP), AX.X,
                                        ALU.add).then_inc(q_summed, 1)

            def o_lo_out(t, j):
                dve.wait_ge(o_hi, 2 * t + j)
                rest(ot[:, 1].rearrange("p h n -> p (h n)"), bO[:, :],
                     ot[:, 0].rearrange("p h n -> p (h n)")).then_inc(o_lo, 1)

            def probs_lo(t, j, k):
                g = 2 * t + j
                dve.wait_ge(p_hi, UNITS * g + k + 1)
                c = slice(k * 512, (k + 1) * 512)
                rest(pt[:, 1].rearrange("p h t n -> p (h t n)")[:, c], bT[(j + k) % 2][:, :],
                     pt[:, 0].rearrange("p h t n -> p (h t n)")[:, c]).then_inc(p_lo, 1)

            def k_rope(t, j):
                n, m = 2 * t + j + 1, (j + 1) % 2
                dve.wait_ge(rk_ready, n + 1)
                wait(dve, kT_done, n)
                nc.vector.scalar_tensor_tensor(kr1, ks[:, 0:HD], rk, rope[:, m, 2 * HD:3 * HD], ALU.mult, ALU.mult)
                nc.vector.scalar_tensor_tensor(kr2, ks[:, 0:HD], rk, rope[:, m, 3 * HD:4 * HD], ALU.mult,
                                               ALU.mult).then_inc(k_mul, 1)
                dve.wait_ge(k_mul, n + 1)
                h = HD // 2
                nc.vector.tensor_tensor(kr[:, 0:h], kr1[:, 0:h], kr2[:, h:HD], ALU.add)
                nc.vector.tensor_tensor(kr[:, h:HD], kr1[:, h:HD], kr2[:, 0:h], ALU.add).then_inc(kr_ready, 1)

            def q_T_lo(t, j):
                n, m = 2 * t + j + 1, (j + 1) % 2
                dve.wait_ge(qT_hi, n + 1)
                rest(qT[:, m, 1].rearrange("p h n -> p (h n)"), bW[:, :],
                     qT[:, m, 0].rearrange("p h n -> p (h n)")).then_inc(qT_lo, 1)

            def add_out(t, j):
                f = 2 * t + j - 1
                dve.wait_ge(wo_done, f + 1)
                row = acc[:, at(f % ROWS), :].rearrange("p a n -> p (a n)")
                nc.vector.tensor_tensor(row, bO[:, :], row, ALU.add).then_inc(added, 1)

            def k_new_lo(t, j, weights):
                n, m = 2 * t + j + 1, (j + 1) % 2
                dve.wait_ge(kn_hi, n + 1)
                if weights:
                    dve.wait_ge(wkv_hi, t + 1)
                rest(kT[:, m, 1, CACHE:KEYS], bQ[:, 0:P], kT[:, m, 0, CACHE:KEYS]).then_inc(kn_lo, 1)

            def wkv_rest(t):
                dve.wait_ge(wkv_hi, t + 1)
                rest(tile_of(wkvT, t, 1), bQ[:, P:3 * P], tile_of(wkvT, t, 0)).then_inc(wkv_lo, 1)

            def w_rest(t, j):
                dve.wait_ge(wo_hi if j else wq_hi, t + 1)
                w = woT if j else wqT
                rest(columns_of(w, t, 1), bW[:, :].rearrange("p (c n) -> p c n", c=4),
                     columns_of(w, t, 0)).then_inc(wo_lo if j else wq_lo, 1)

            def turn(t, first=False, last=False):
                for j in range(2):
                    prev, nxt, weights = not (first and j == 0), not (last and j == 1), not last
                    head_max(t, j, 0)
                    if nxt:
                        k_cache_lo(t, j)
                    head_sum(t, j, 0)
                    if nxt:
                        make_mask(t, j)
                    head_max(t, j, 1)
                    if nxt:
                        q_sum(t, j)
                    head_sum(t, j, 1)
                    if prev:
                        o_lo_out(t, j)
                    head_max(t, j, 2)
                    if nxt:
                        values_cache_lo(t, j)
                    probs_lo(t, j, 0)
                    head_sum(t, j, 2)
                    head_max(t, j, 3)
                    if nxt:
                        k_rope(t, j)
                    probs_lo(t, j, 1)
                    if nxt:
                        q_T_lo(t, j)
                    head_sum(t, j, 3)
                    if prev:
                        add_out(t, j)
                    if nxt:
                        k_new_lo(t, j, j == 0 and weights)
                        if j == 0 and weights:
                            wkv_rest(t)
                    probs_lo(t, j, 2)
                    if weights:
                        w_rest(t, j)
                    probs_lo(t, j, 3)
                    probs_lo(t, j, 4)

            k_cache_lo(-1, 1)
            dve.wait_ge(pool_step, 2)
            make_mask(-1, 1)
            q_sum(-1, 1)
            values_cache_lo(-1, 1)
            k_rope(-1, 1)
            q_T_lo(-1, 1)
            k_new_lo(-1, 1, False)
            turn(0, first=True)
            with dve.Fori(1, TURNS - 1) as t:
                turn(t)
            turn(TURNS - 1, last=True)
            o_lo_out(TURNS, 0)
            add_out(TURNS, 0)

        @block.gpsimd
        def _(pool):
            key_rows = kc.rearrange("g s h d -> (g s h) d")
            value_rows = vc.rearrange("g s h d -> (g s h) d")
            nc.gpsimd.iota(tok8, [[0, 1]], base=0, channel_multiplier=KVH, allow_small_or_imprecise_dtypes=True)
            nc.gpsimd.iota(tokf, [[0, 1]], base=0, channel_multiplier=1,
                           allow_small_or_imprecise_dtypes=True).then_inc(const_ready, 1)
            nc.gpsimd.memset(ident[:, :], 0.0).then_inc(pool_step, 1)
            pool.wait_ge(pool_step, 1)
            nc.gpsimd.affine_select(out=ident[:, :], in_=ident[:, :], compare_op=ALU.not_equal, fill=1.0, base=0,
                                    pattern=[[-1, P]], channel_multiplier=1).then_inc(ident_ready, 1)
            nc.gpsimd.memset(half, -0.5)
            nc.gpsimd.memset(one4, 1.0)
            nc.gpsimd.memset(mask[:, :, CACHE:KEYS], 0.0)
            rev, num = gwork[:, 4, :], gwork[:, 5, :]
            nc.gpsimd.iota(rev, [[0, ROWS], [-1, EXPERTS]], base=EXPERTS, channel_multiplier=0,
                           allow_small_or_imprecise_dtypes=True)
            nc.gpsimd.iota(num, [[0, ROWS], [1, EXPERTS]], base=0, channel_multiplier=0,
                           allow_small_or_imprecise_dtypes=True).then_inc(experts_ready, 1)
            pool.wait_ge(wn_ready, 1)
            pool.wait_ge(sin_ready, 1)
            pool.wait_ge(cos_ready, 1)
            h = HD // 2
            for i in range(4):
                if i >= 2:
                    pool.wait_ge(comp_out[i % 2], 16)
                wave = (cost, sint)[i % 2].rearrange("p (b n) -> p b n", b=ROWS)
                weight = wn[:, (0, 1, 2, 3)[i], :]
                for s in range(2):
                    last = nc.gpsimd.tensor_tensor(
                        comp[i % 2][:, :, s * h:(s + 1) * h], wave,
                        weight[:, s * h:(s + 1) * h].unsqueeze(1).to_broadcast([P, ROWS, h]), ALU.mult)
                last.then_inc(comp_ready, 1)
            pool.wait_ge(comp_ready, 4)
            nc.gpsimd.iota(keyno[:, :], [[1, CACHE]], base=0, channel_multiplier=0,
                           allow_small_or_imprecise_dtypes=True).then_inc(pool_step, 1)
            with pool.Fori(0, PAIRS) as u:
                for j in range(2):
                    pool.wait_ge(c_x1, 2 * u + j + 1)
                    hold(pool)
                    nc.gpsimd.tensor_copy(acc[:, bass.ds(2 * u + j, 1), :], x1[j].unsqueeze(1)).then_inc(c_acc, 1)

            def gather_keys(b, j, k):
                gk = 2 * k + j
                pool_row = pageidx[:, at(b), :].rearrange("p a c -> p (a c)")
                wait(pool, idx_step, 1 + 2 * gk)
                hold(pool)
                nc.gpsimd.tensor_copy(kidx[:, j, :], pool_row).then_inc(idx_step, 1)
                wait(pool, idx_step, 2 + 2 * gk)
                hold(pool)
                nc.gpsimd.tensor_tensor(pool_row, pool_row, one4, ALU.add).then_inc(idx_step, 1)
                for c in range(CT):
                    nc.gpsimd.indirect_dma_start(
                        kraw[:, j, c, :], None, key_rows,
                        bass.IndirectOffsetOnAxis(ap=kidx[:, j, c:c + 1], axis=0)).then_inc(k_in[j], 16)

            def gather_values(j):
                for c in range(CT):
                    nc.gpsimd.indirect_dma_start(
                        vraw[:, j, c, :], None, value_rows,
                        bass.IndirectOffsetOnAxis(ap=kidx[:, j, c:c + 1], axis=0)).then_inc(v_in[j], 16)

            def q_rope(t, j):
                n, m, uses = 2 * t + j + 1, (j + 1) % 2, t + 1 + j
                q3, a3, b3, r3 = (v.rearrange("p (h n) -> p h n", h=REP) for v in (qs, u1, u2, qr))
                pool.wait_ge(rope_in[m], 16 * uses)
                pool.wait_ge(q_copied, n + 1)
                hold(pool)
                nc.gpsimd.tensor_tensor(a3, q3, rope[:, m, 0:HD].unsqueeze(1).to_broadcast([P, REP, HD]), ALU.mult)
                nc.gpsimd.tensor_tensor(b3, q3, rope[:, m, HD:2 * HD].unsqueeze(1).to_broadcast([P, REP, HD]),
                                        ALU.mult).then_inc(q_mul, 1)
                pool.wait_ge(q_mul, n + 1)
                wait(pool, qT_done, n)
                nc.gpsimd.tensor_tensor(r3[:, :, 0:h], a3[:, :, 0:h], b3[:, :, h:HD], ALU.add)
                nc.gpsimd.tensor_tensor(r3[:, :, h:HD], a3[:, :, h:HD], b3[:, :, 0:h], ALU.add).then_inc(qr_ready, 1)

            def q_scale(t, j):
                n, m = 2 * t + j + 1, (j + 1) % 2
                pool.wait_ge(q_summed, n + 1)
                hold(pool)
                nc.gpsimd.tensor_scalar(ssq[:, m, :], ssq[:, m, :], HD * EPS, None, ALU.add).then_inc(rq_arg, 1)
                pool.wait_ge(rq_arg, n + 1)
                nc.gpsimd.tensor_tensor(rq[:, m, :], ssq[:, m, :], half, ALU.pow).then_inc(rq_ready, 1)

            def kv_new(t, j):
                n, m = 2 * t + j + 1, (j + 1) % 2
                pool.wait_ge(k_squared, n + 1)
                wait(pool, k_mul, n)
                hold(pool)
                nc.gpsimd.tensor_scalar(ssk1, ssk, HD * EPS, None, ALU.add).then_inc(rk_arg, 1)
                pool.wait_ge(rk_arg, n + 1)
                nc.gpsimd.tensor_tensor(rk, ssk1, half[:, 0:1], ALU.pow).then_inc(rk_ready, 1)
                pool.wait_ge(vn_hi, n + 1)
                nc.gpsimd.tensor_tensor(vs[:, m, 1, CT, :], ks[:, HD:2 * HD], vs[:, m, 0, CT, :].bitcast(FP32),
                                        ALU.subtract).then_inc(vn_split, 1)

            def turn(t, last=False):
                for j in range(2):
                    nxt = not (last and j == 1)
                    if not last:
                        wait(pool, kc_done, 2 * t + j + 1)
                        gather_keys(((t + 1) % PAIRS) * 2 + j, j, t + 1)
                    if nxt:
                        q_rope(t, j)
                        q_scale(t, j)
                        kv_new(t, j)
                    if not last:
                        wait(pool, vc_split, 2 * t + j + 1)
                        hold(pool)
                        gather_values(j)

            pool.wait_ge(pool_step, 2)
            pool.wait_ge(prep_T, NPREP)
            gather_keys(0, 0, 0)
            gather_values(0)
            gather_keys(1, 1, 0)
            gather_values(1)
            q_rope(-1, 1)
            q_scale(-1, 1)
            kv_new(-1, 1)
            turn(0)
            with pool.Fori(1, TURNS - 1) as t:
                turn(t)
            turn(TURNS - 1, last=True)


INPUTS = ["x", "itok_B_0_7", "itok_Bx16_0_63", "itok_B_207_1644", "L0_cond_W", "L0_cond_Wr", "L0_cond_A", "L0_cond_B",
          "L1_cond_Wq", "L1_cond_Wk", "L1_cond_Wv", "L1_cond_Wo", "L1_cond_q_norm_w", "L1_cond_k_norm_w",
          "L1_cond_k_cache", "L1_cond_v_cache"]


def kernel(**inputs):
    import concourse.bacc as bacc
    from concourse.bass_utils import run_bass_kernel_spmd

    nc = bacc.Bacc("TRN2", target_bir_lowering=False, num_devices=1)
    arrays, args = {}, []
    for name in INPUTS:
        a = np.ascontiguousarray(inputs[name])
        arrays[f"in_{name}"] = a
        args.append(nc.dram_tensor(f"in_{name}", a.shape, mybir.dt.from_np(a.dtype), kind="ExternalInput").ap())
    inv = (1.0 / 10000.0 ** (np.arange(0, HD, 2, dtype=np.float64) / HD)).astype(np.float32)
    arrays["inv_freq"] = inv
    args.append(nc.dram_tensor("inv_freq", inv.shape, FP32, kind="ExternalInput").ap())
    out = nc.dram_tensor("out", (ROWS, P, DM), FP32, kind="ExternalOutput").ap()
    build(nc, *args, out)
    return run_bass_kernel_spmd(nc, [arrays], core_ids=[0]).results[0]["out"]
```

```python
import math
from contextlib import ExitStack

import concourse.bass as bass
import numpy as np
from concourse import mybir

FP32 = mybir.dt.float32
FP32R = mybir.dt.float32r
I32 = mybir.dt.int32
U32 = mybir.dt.uint32
ALU = mybir.AluOpType
ACT = mybir.ActivationFunctionType
AX = mybir.AxisListType

P = 128
ROWS, DM = 8, 512
KT = DM // P
EXPERTS, RANK = 8, 16
ER = EXPERTS * RANK
HD = 128
KVH, REP = 8, 4
QW = REP * HD
PAGE, NPP = 32, 16
CACHE = PAGE * NPP
KEYS = CACHE + P
TILES = KEYS // P
CT = CACHE // P
GROUPS = KVH * ROWS
TURNS = GROUPS // 2
PAIRS = ROWS // 2
UNITS = REP * TILES // 4
CTX = 4 * HD + 32
HL = ER + EXPERTS
EPS = 1e-6
NEG = -1e30
LANG_BIAS = 5.0
LORA_SCALE = 2.0
TWO_PI = 2 * math.pi
ROUND = 1.5 * 2.0 ** 23


def two_pi_parts():
    a = round(TWO_PI * 64) / 64
    b = round((TWO_PI - a) * 2 ** 17) / 2 ** 17
    return a, b, TWO_PI - a - b


def build(nc, x, lang, table, lens, w0, wr, la, lb, wq, wk, wv, wo, qn, kn, kc, vc, invf, out):
    ctx = ExitStack()
    with ctx:
        def sb(name, shape, dt=FP32):
            return ctx.enter_context(nc.sbuf_tensor(name, shape, dt))

        def ps(name, shape):
            return ctx.enter_context(nc.psum_tensor(name, shape, FP32))

        def sem(name):
            return ctx.enter_context(nc.semaphore(name))

        wqT = sb("wqT", [P, 2, 2, KT, QW], FP32R)
        wkvT = sb("wkvT", [P, 2, 2, KT, 2 * HD], FP32R)
        woT = sb("woT", [P, 2, 2, REP, DM], FP32R)
        xs = sb("xs", [P, 2, 2, KT, P], FP32R)
        rope = sb("rope", [P, 2, CTX])
        kraw = sb("kraw", [P, 2, CT, HD])
        vraw = sb("vraw", [P, 2, CT, HD])
        kT = sb("kT", [P, 2, 2, KEYS], FP32R)
        vs = sb("vs", [P, 2, 2, TILES, HD], FP32R)
        qT = sb("qT", [P, 2, 2, REP, P], FP32R)
        pr = sb("pr", [P, REP, KEYS])
        pt = sb("pt", [P, 2, REP, TILES, P], FP32R)
        ot = sb("ot", [P, 2, REP, P], FP32R)
        mask = sb("mask", [P, 2, KEYS])
        qwork = sb("qwork", [P, 5, QW])
        kwork = sb("kwork", [P, 6, HD])
        wraw = sb("wraw", [P, 2, QW + 2 * HD])
        acc = sb("acc", [P, ROWS, DM])
        ident = sb("ident", [P, P])
        keyno = sb("keyno", [P, CACHE])
        pageidx = sb("pageidx", [P, ROWS, CT])
        kidx = sb("kidx", [P, 2, CT], U32)
        tab = sb("tab", [P, ROWS * NPP], I32)
        small = sb("small", [P, 128])
        qs, sq, u1, u2, qr = (qwork[:, i, :] for i in range(5))
        ks = kwork[:, 0:2, :].rearrange("p a n -> p (a n)")
        kr1, kr2, kr, ksq = (kwork[:, i, :] for i in range(2, 6))
        maxs, nbias, sums, rinv = (small[:, 4 * i:4 * i + 4] for i in range(4))
        ssq = small[:, 16:24].rearrange("p (j h) -> p j h", j=2)
        rq = small[:, 24:32].rearrange("p (j h) -> p j h", j=2)
        ssk, rk, half = small[:, 32:33], small[:, 33:34], small[:, 36:40]
        ssk1 = small[:, 34:35]
        one4 = small[:, 40:44]
        tok8 = small[:, 44:45]
        tokf = small[:, 45:46]
        lenf = small[:, 48:56]
        langf = small[:, 56:64]
        ints = small[:, 64:80].bitcast(I32)
        posf = small[:, 80:88]
        m1, m2, top1, p1, p2 = (small[:, 88 + 8 * i:96 + 8 * i] for i in range(5))
        w0T = wqT[:, 1]
        raT = wkvT[:, 1].rearrange("p a t n -> p (a t n)")[:, 0:2 * KT * HL].rearrange(
            "p (a t n) -> p a t n", a=2, t=KT)
        lbT = woT[:, 1, :, 0, :]
        hgT = woT[:, 1, :, 1, 0:2 * P].rearrange("p a (j n) -> p j a n", j=2)
        x0 = mask
        hl = rope[:, :, :].rearrange("p j n -> p (j n)")[:, 0:ROWS * HL].rearrange("p (b n) -> p b n", b=ROWS)
        gwork = kwork[:, :, :].rearrange("p a n -> p (a n)").rearrange("p (a n) -> p a n", n=ROWS * EXPERTS)
        hg = [ot[:, 0, 0, :], ot[:, 0, 1, :]]
        x1 = [qwork[:, 3, :], qwork[:, 4, :]]
        ang, turns, sint, cost = (qwork[:, i, :] for i in range(4))
        comp = [pr[:, 2 * i:2 * i + 2, :].rearrange("p a n -> p (a n)")[:, 0:ROWS * HD].rearrange(
            "p (b n) -> p b n", b=ROWS) for i in range(2)]
        wn = keyno[:, :].rearrange("p (a n) -> p a n", a=4)
        hgb = sb("hgb", [P, 2, P])

        xT_d = nc.dram_tensor("xT_scratch", (ROWS, P, 2 * KT * P), FP32, kind="Internal").ap()
        rope_d = nc.dram_tensor("rope_scratch", (ROWS, P, CTX), FP32, kind="Internal").ap()

        bS = ps("bS", [P, 1024])[:, 0:KEYS]
        bT = [ps("bT0", [P, 512]), ps("bT1", [P, 512])]
        bQ, bK, bO, bW = (ps(n, [P, 512]) for n in ("bQ", "bK", "bO", "bW"))

        scores_done, kc_done, q_done, kv_done = (sem(n) for n in ("scores_done", "kc_done", "q_done", "kv_done"))
        qT_done, kT_done, pT_done, pv_done, wo_done = (
            sem(n) for n in ("qT_done", "kT_done", "pT_done", "pv_done", "wo_done"))
        wqT_done, woT_done = sem("wqT_done"), sem("woT_done")
        kc_hi, kc_lo, kn_hi, kn_lo, qT_hi, qT_lo = (
            sem(n) for n in ("kc_hi", "kc_lo", "kn_hi", "kn_lo", "qT_hi", "qT_lo"))
        p_hi, p_lo, o_hi, o_lo = (sem(n) for n in ("p_hi", "p_lo", "o_hi", "o_lo"))
        wq_hi, wq_lo, wkv_hi, wkv_lo, wo_hi, wo_lo = (
            sem(n) for n in ("wq_hi", "wq_lo", "wkv_hi", "wkv_lo", "wo_hi", "wo_lo"))
        q_copied, q_squared, q_summed, rq_ready, qr_ready = (
            sem(n) for n in ("q_copied", "q_squared", "q_summed", "rq_ready", "qr_ready"))
        kv_copied, k_squared, rk_ready, kr_ready = (
            sem(n) for n in ("kv_copied", "k_squared", "rk_ready", "kr_ready"))
        max_done, bias_ready, exp_done, rinv_ready, norm_act, norm_dve = (
            sem(n) for n in ("max_done", "bias_ready", "exp_done", "rinv_ready", "norm_act", "norm_dve"))
        mask_ready, vc_split, vn_split, added = (sem(n) for n in ("mask_ready", "vc_split", "vn_split", "added"))
        x_in, rope_in, k_in, v_in, w_in = ([sem(f"{n}{j}") for j in range(2)] for n in
                                           ("x_in", "rope_in", "k_in", "v_in", "w_in"))
        held = sem("held")
        dve_step, pool_step, act_step = sem("dve_step"), sem("pool_step"), sem("act_step")
        rq_arg, rk_arg, q_mul, k_mul, vc_hi, vn_hi = (
            sem(n) for n in ("rq_arg", "rk_arg", "q_mul", "k_mul", "vc_hi", "vn_hi"))
        lens_ready = sem("lens_ready")
        consts_in, ident_ready, const_ready = sem("consts_in"), sem("ident_ready"), sem("const_ready")
        idx_step = sem("idx_step")
        prep_in = [sem(f"prep_in{i}") for i in range(6)]
        prep_T, prep_hi, prep_lo = sem("prep_T"), sem("prep_hi"), sem("prep_lo")
        acc_in, tile_in = sem("acc_in"), [sem("tile_in0"), sem("tile_in1")]
        a_T, a_hi, a_lo, a_proj, a_hl, a_add = (sem(n) for n in ("a_T", "a_hi", "a_lo", "a_proj", "a_hl", "a_add"))
        experts_ready, diff_ready, wn_ready = sem("experts_ready"), sem("diff_ready"), sem("wn_ready")
        c_hg, c_T, c_hi, c_lo, c_lora, c_x1, c_acc, c_xT, c_xhi, c_xlo = (
            sem(n) for n in ("c_hg", "c_T", "c_hi", "c_lo", "c_lora", "c_x1", "c_acc", "c_xT", "c_xhi", "c_xlo"))
        c_out = [sem("c_out0"), sem("c_out1")]
        angle_ready, sin_ready, cosarg_ready, cos_ready = (
            sem(n) for n in ("angle_ready", "sin_ready", "cosarg_ready", "cos_ready"))
        comp_ready, comp_out, lens_out = sem("comp_ready"), [sem("comp_out0"), sem("comp_out1")], sem("lens_out")
        out_stored = sem("out_stored")

        def wait(eng, s, n):
            if not isinstance(n, int) or n > 0:
                eng.wait_ge(s, n)

        def hold(eng):
            eng.sem_inc(held, 1)

        prep = []
        for ot_ in range(KT):
            prep.append((w0[ot_ * P:(ot_ + 1) * P, :], P, [w0T[:, a, :, ot_ * P:(ot_ + 1) * P] for a in range(2)]))
        prep.append((la.rearrange("e r d -> (e r) d"), P, [raT[:, a, :, 0:ER] for a in range(2)]))
        prep.append((wr, EXPERTS, [raT[:, a, :, ER:HL] for a in range(2)]))
        prep.append((None, P, [lbT[:, a, :].rearrange("p (t n) -> p t n", t=KT) for a in range(2)]))
        for e in range(REP):
            prep.append((wq[e * P:(e + 1) * P, :], P, [wqT[:, 0, a, :, e * P:(e + 1) * P] for a in range(2)]))
        prep.append((wk[0:HD, :], P, [wkvT[:, 0, a, :, 0:HD] for a in range(2)]))
        prep.append((wv[0:HD, :], P, [wkvT[:, 0, a, :, HD:2 * HD] for a in range(2)]))
        for o in range(KT):
            prep.append((wo[o * P:(o + 1) * P, 0:QW], P, [woT[:, 0, a, :, o * P:(o + 1) * P] for a in range(2)]))
        NPREP = len(prep)
        loads = [EXPERTS if w[0] is None else 1 for w in prep]
        prep_count = [16 * sum(loads[i % 6:i + 1:6]) for i in range(NPREP)]
        N0 = 7
        stage = [kraw[:, 0].rearrange("p t n -> p (t n)"), kraw[:, 1].rearrange("p t n -> p (t n)"),
                 vraw[:, 0].rearrange("p t n -> p (t n)"), vraw[:, 1].rearrange("p t n -> p (t n)"),
                 wraw[:, 0, 0:QW], wraw[:, 1, 0:QW]]
        prep_bank = [bW, bK]

        def at(i, n=1):
            return slice(i * n, (i + 1) * n) if isinstance(i, int) else bass.ds(i * n, n)

        def part_of(view, kv, a, tile):
            return view[:, at(kv % 2), a, tile, :].rearrange("p k n -> p (k n)")

        def columns_of(view, t, a):
            return view[:, at((t // PAIRS + 1) % 2), a, :, at(t % PAIRS, P)].rearrange("p k t n -> p (k t) n")

        def tile_of(view, t, a):
            return view[:, at((t // PAIRS + 1) % 2), a, at(t % PAIRS), :].rearrange("p k t n -> p (k t n)")

        def there(t, j, d):
            return not isinstance(t, int) or 0 <= 2 * t + j + d < GROUPS

        def weights(t):
            return not isinstance(t, int) or 0 <= t < TURNS - 1

        def kv_of_next(t, j):
            return t // PAIRS if j == 0 else (t + 1) // PAIRS

        def kv_of_last(t, j):
            return (t - 1) // PAIRS if j == 0 else t // PAIRS

        block = ctx.enter_context(nc.Block())

        @block.sync
        def _(sp):
            sp.dma_start(tab[:, :], table.rearrange("b n -> (b n)").partition_broadcast(P)).then_inc(consts_in, 16)
            sp.dma_start(ints[:, 0:8], lens.partition_broadcast(P)).then_inc(consts_in, 16)
            sp.dma_start(ints[:, 8:16], lang.partition_broadcast(P)).then_inc(consts_in, 16)
            sp.dma_start(wn[:, 0, :], qn.partition_broadcast(P)).then_inc(consts_in, 16)
            sp.dma_start(wn[:, 2, :], kn.partition_broadcast(P)).then_inc(consts_in, 16)
            sp.dma_start(wn[:, 1, 0:HD // 2], invf.partition_broadcast(P)).then_inc(consts_in, 16)

            def load_weight(i):
                src, n, _ = prep[i]
                if i >= 6:
                    sp.wait_ge(prep_T, i - 5)
                dst = stage[i % 6]
                if src is None:
                    for e in range(EXPERTS):
                        d = dst.rearrange("p (t e r) -> p t e r", t=KT, e=EXPERTS)[:, :, e, :]
                        sp.dma_start(d, lb[e].rearrange("(t p) r -> p t r", p=P)).then_inc(prep_in[i % 6], 16)
                else:
                    sp.dma_start(dst[0:n, :], src).then_inc(prep_in[i % 6], 16)

            def load_tile(b, j, k):
                wait(sp, a_T, b - 1)
                sp.dma_start(x0[:, j, 0:DM], x[at(b)].rearrange("a p n -> p (a n)")).then_inc(tile_in[j], 16)

            load_tile(0, 0, 0)
            load_tile(1, 1, 0)
            for i in range(6):
                load_weight(i)
            sp.dma_start(acc[:, :, :], x.rearrange("b p n -> p b n")).then_inc(acc_in, 16)
            for i in range(6, N0):
                load_weight(i)
            for b in range(2, ROWS):
                load_tile(b, b % 2, b // 2)
                load_weight(N0 + b - 2)
            for i in range(N0 + ROWS - 2, NPREP):
                load_weight(i)

            for i in range(4):
                sp.wait_ge(comp_ready, i + 1)
                sp.dma_start(rope_d[:, :, i * HD:(i + 1) * HD].rearrange("b p n -> p b n"),
                             comp[i % 2]).then_inc(comp_out[i % 2], 16)
            sp.wait_ge(lens_ready, 1)
            sp.dma_start(rope_d[:, :, 4 * HD:4 * HD + 1].rearrange("b p n -> p b n"),
                         lenf.unsqueeze(2), allow_slow_non_contiguous=True).then_inc(lens_out, 16)
            with sp.Fori(0, PAIRS) as u:
                for j in range(2):
                    sp.wait_ge(c_xlo, 2 * u + j + 1)
                    sp.dma_start(xT_d[bass.ds(2 * u + j, 1)].rearrange("a p n -> p (a n)"),
                                 xs[:, j].rearrange("p a t n -> p (a t n)").bitcast(FP32)).then_inc(c_out[j], 16)
            sp.wait_ge(c_out[0], 16 * PAIRS)
            sp.wait_ge(c_out[1], 16 * PAIRS)
            sp.wait_ge(comp_out[0], 32)
            sp.wait_ge(comp_out[1], 32)
            sp.wait_ge(lens_out, 16)
            sp.wait_ge(prep_T, NPREP)

            def load_group(b, j):
                sp.dma_start(xs[:, j].rearrange("p a t n -> p (a t n)").bitcast(FP32),
                             xT_d[at(b)].rearrange("a p n -> p (a n)")).then_inc(x_in[j], 16)
                sp.dma_start(rope[:, j, 0:4 * HD + 1],
                             rope_d[at(b), :, 0:4 * HD + 1].rearrange("a p n -> p (a n)")).then_inc(rope_in[j], 16)

            def load_weights(j, kv, part):
                if j == 0:
                    sp.dma_start(wraw[:, 0, 0:QW], wq[at(kv * REP + part, P), :]).then_inc(w_in[0], 16)
                    sp.dma_start(wraw[:, 0, QW:QW + HD], wk[at(kv, HD), at(part, P)]).then_inc(w_in[0], 16)
                    sp.dma_start(wraw[:, 0, QW + HD:QW + 2 * HD], wv[at(kv, HD), at(part, P)]).then_inc(w_in[0], 16)
                else:
                    sp.dma_start(wraw[:, 1, 0:QW], wo[at(part, P), at(kv, QW)]).then_inc(w_in[1], 16)

            def turn(t, store):
                for j in range(2):
                    g = 2 * t + j
                    wait(sp, kv_done, g + 1)
                    wait(sp, q_mul, g + 1)
                    wait(sp, k_mul, g + 1)
                    wait(sp, mask_ready, g + 1)
                    load_group(((t + 1) % PAIRS) * 2 + j, j)
                    u = t if j == 0 else t + 1
                    if j == 0:
                        wait(sp, woT_done, t)
                        load_weights(1, (u // PAIRS + 1) % KVH, u % PAIRS)
                    else:
                        wait(sp, wqT_done, t + 1)
                        wait(sp, kT_done, 2 * t + 2)
                        load_weights(0, (u // PAIRS + 1) % KVH, u % PAIRS)
                    if store:
                        store_row(g - 2)

            def store_row(g):
                sp.wait_ge(added, g + 1)
                b = g % ROWS
                sp.dma_start(out[at(b)].rearrange("a p n -> p (a n)"),
                             acc[:, at(b), :].rearrange("p a n -> p (a n)")).then_inc(out_stored, 16)

            load_group(0, 0)
            load_group(1, 1)
            load_weights(0, 1, 0)
            turn(0, False)
            with sp.Fori(1, TURNS - 3) as t:
                turn(t, False)
            with sp.Fori(TURNS - 3, TURNS - 1) as t:
                turn(t, True)
            for g in range(GROUPS - 4, GROUPS):
                store_row(g)
            sp.wait_ge(out_stored, 16 * ROWS)

        @block.tensor
        def _(pe):
            def mm3(dst, lhs, rhs, first, last):
                nc.tensor.matmul(dst, lhs[0], rhs[0], start=first, stop=False)
                nc.tensor.matmul(dst, lhs[0], rhs[1], start=False, stop=False)
                return nc.tensor.matmul(dst, lhs[1], rhs[0], start=False, stop=last)

            pe.wait_ge(ident_ready, 1)

            def prep_unit(i):
                _, n, _ = prep[i]
                pe.wait_ge(prep_in[i % 6], prep_count[i])
                if i >= 2:
                    pe.wait_ge(prep_lo, i - 1)
                bank = prep_bank[i % 2]
                for c in range(KT):
                    src = stage[i % 6][0:n, c * P:(c + 1) * P]
                    last = nc.tensor.transpose(bank[:, c * n:(c + 1) * n], src, ident[0:n, 0:n])
                last.then_inc(prep_T, 1)

            for i in range(N0):
                prep_unit(i)

            with pe.Fori(0, PAIRS) as u:
                for j in range(2):
                    pe.wait_ge(tile_in[j], 16 * u + 16)
                    if j == 0:
                        pe.wait_ge(prep_lo, N0)
                    for c in range(KT):
                        last = nc.tensor.transpose(prep_bank[j][:, c * P:(c + 1) * P], x0[:, j, c * P:(c + 1) * P],
                                                   ident[:, :])
                    last.then_inc(a_T, 1)
                for j in range(2):
                    b = 2 * u + j
                    pe.wait_ge(a_lo, b + 1)
                    for c in range(KT):
                        mm3(bT[j][:, :], [xs[:, j, a, c, :] for a in range(2)],
                            [w0T[:, a, c, :] for a in range(2)], c == 0, c == KT - 1)
                    for c in range(KT):
                        last = mm3([bQ, bO][j][:, 0:HL], [xs[:, j, a, c, :] for a in range(2)],
                                   [raT[:, a, c, :] for a in range(2)], c == 0, c == KT - 1)
                    last.then_inc(a_proj, 1)
                pe.wait_ge(a_add, 2 * u + 2)
                pe.wait_ge(a_hl, 2 * u + 2)

            for i in range(N0, NPREP):
                prep_unit(i)
            pe.wait_ge(prep_lo, NPREP)
            with pe.Fori(0, PAIRS) as u:
                for j in range(2):
                    pe.wait_ge(c_hg, 2 * u + j + 1)
                    nc.tensor.transpose(prep_bank[j][:, 0:P], hgb[:, j, :], ident[:, :]).then_inc(c_T, 1)
                for j in range(2):
                    pe.wait_ge(c_lo, 2 * u + j + 1)
                    mm3(bT[j][:, :], [hgT[:, j, a, :] for a in range(2)], [lbT[:, a, :] for a in range(2)],
                        True, True).then_inc(c_lora, 1)
                for j in range(2):
                    pe.wait_ge(c_x1, 2 * u + j + 1)
                    for c in range(KT):
                        last = nc.tensor.transpose([bQ, bO][j][:, c * P:(c + 1) * P], x1[j][:, c * P:(c + 1) * P],
                                                   ident[:, :])
                    last.then_inc(c_xT, 1)
                pe.wait_ge(c_xlo, 2 * u + 2)

            def scores(t, j, h):
                g = 2 * t + j
                if h == 0:
                    pe.wait_ge(kc_lo, g + 1)
                    pe.wait_ge(kn_lo, g + 1)
                    pe.wait_ge(qT_lo, g + 1)
                wait(pe, max_done, 4 * g + h)
                qh = [qT[:, j, a, h, :] for a in range(2)]
                mm3(bS[:, 0:CACHE], qh, [kT[:, j, a, 0:CACHE] for a in range(2)], True, True)
                mm3(bS[:, CACHE:KEYS], qh, [kT[:, j, a, CACHE:KEYS] for a in range(2)],
                    True, True).then_inc(scores_done, 1)

            def k_cache_T(t, j):
                n = 2 * t + j + 2
                wait(pe, vn_hi, n)
                pe.wait_ge(k_in[j], 16 * CT * (t + 2))
                for c in range(CT):
                    last = nc.tensor.transpose(bK[:, c * P:(c + 1) * P], kraw[:, j, c, :], ident[:, :])
                last.then_inc(kc_done, 1)

            def q_proj(t, j):
                n, m, uses, kv = 2 * t + j + 1, (j + 1) % 2, t + 1 + j, kv_of_next(t, j)
                wait(pe, kn_lo, n)
                pe.wait_ge(x_in[m], 16 * uses)
                if j == 1:
                    wait(pe, wkv_lo, t + 1)
                    wait(pe, wq_lo, t + 1)
                for c in range(KT):
                    last = mm3(bQ[:, :], [xs[:, m, a, c, :] for a in range(2)],
                               [part_of(wqT, kv, a, c) for a in range(2)], c == 0, c == KT - 1)
                last.then_inc(q_done, 1)

            def kv_proj(t, j):
                n, m, kv = 2 * t + j + 1, (j + 1) % 2, kv_of_next(t, j)
                pe.wait_ge(kc_lo, n + 1)
                for c in range(KT):
                    last = mm3(bK[:, 0:2 * HD], [xs[:, m, a, c, :] for a in range(2)],
                               [part_of(wkvT, kv, a, c) for a in range(2)], c == 0, c == KT - 1)
                last.then_inc(kv_done, 1)

            def q_T(t, j):
                n = 2 * t + j + 1
                pe.wait_ge(qr_ready, n + 1)
                wait(pe, wq_lo if j else wo_lo, t + 1 if j else t)
                for h in range(REP):
                    last = nc.tensor.transpose(bW[:, h * P:(h + 1) * P], qr[:, h * P:(h + 1) * P], ident[:, :])
                last.then_inc(qT_done, 1)

            def k_new_T(t, j):
                n = 2 * t + j + 1
                pe.wait_ge(kr_ready, n + 1)
                pe.wait_ge(q_copied, n + 1)
                last = nc.tensor.transpose(bQ[:, 0:P], kr, ident[:, :])
                if j == 0 and weights(t):
                    pe.wait_ge(w_in[0], 48 * (t + 1))
                    for i in range(2):
                        last = nc.tensor.transpose(bQ[:, (1 + i) * P:(2 + i) * P],
                                                   wraw[:, 0, QW + i * P:QW + (i + 1) * P], ident[:, :])
                last.then_inc(kT_done, 1)

            def w_T(t, j):
                pe.wait_ge(w_in[j], (48 if j == 0 else 16) * (t + 1))
                pe.wait_ge(qT_lo, 2 * t + j + 2)
                for c in range(4):
                    last = nc.tensor.transpose(bW[:, c * P:(c + 1) * P], wraw[:, j, c * P:(c + 1) * P], ident[:, :])
                last.then_inc(woT_done if j else wqT_done, 1)

            def probs_T(t, j, k, d=0):
                g = 2 * t + j + d
                wait(pe, p_lo, UNITS * g + k - 1)
                if k == 1:
                    pe.wait_ge(norm_dve, g + 1)
                else:
                    pe.wait_ge(norm_act, 3 * g + (1, 1, 2, 3, 3)[k])
                for i in range(4):
                    tile = 4 * k + i
                    last = nc.tensor.transpose(bT[(j + d + k) % 2][:, i * P:(i + 1) * P],
                                               pr[:, tile // TILES, (tile % TILES) * P:(tile % TILES + 1) * P],
                                               ident[:, :])
                last.then_inc(pT_done, 1)

            def values(t, j):
                f, m = 2 * t + j - 1, (j + 1) % 2
                wait(pe, added, f)
                pe.wait_ge(p_lo, UNITS * f + UNITS)
                pe.wait_ge(vn_split, f + 1)
                pe.wait_ge(vc_split, f + 1)
                for c in range(TILES):
                    last = mm3(bO[:, :], [vs[:, m, a, c, :] for a in range(2)],
                               [pt[:, a, :, c, :] for a in range(2)], c == 0, c == TILES - 1)
                last.then_inc(pv_done, 1)

            def out_proj(t, j):
                f, kv = 2 * t + j - 1, kv_of_last(t, j)
                pe.wait_ge(o_lo, f + 1)
                for h in range(REP):
                    last = mm3(bO[:, :], [ot[:, a, h, :] for a in range(2)],
                               [part_of(woT, kv, a, h) for a in range(2)], h == 0, h == REP - 1)
                last.then_inc(wo_done, 1)

            def turn(t):
                for j in range(2):
                    this, nxt, prev, after = (there(t, j, d) for d in (0, 1, -1, 2))
                    if this:
                        scores(t, j, 0)
                    if nxt:
                        q_proj(t, j)
                    if this:
                        scores(t, j, 1)
                    if prev:
                        probs_T(t, j, 3, -1)
                        probs_T(t, j, 4, -1)
                    if nxt:
                        kv_proj(t, j)
                    if this:
                        scores(t, j, 2)
                    if prev:
                        values(t, j)
                    if this:
                        probs_T(t, j, 0)
                    if nxt:
                        q_T(t, j)
                    if this:
                        scores(t, j, 3)
                        probs_T(t, j, 1)
                    if prev:
                        out_proj(t, j)
                    if nxt:
                        k_new_T(t, j)
                    if after:
                        k_cache_T(t, j)
                    if weights(t):
                        w_T(t, j)
                    if this:
                        probs_T(t, j, 2)

            turn(-1)
            turn(0)
            with pe.Fori(1, TURNS - 1) as t:
                turn(t)
            turn(TURNS - 1)
            turn(TURNS)

        @block.scalar
        def _(act):
            def take(dst, src):
                return nc.scalar.activation(dst, src, ACT.Copy)

            def prep_take(i):
                _, n, dst = prep[i]
                act.wait_ge(prep_T, i + 1)
                take(dst[0], prep_bank[i % 2][:, 0:KT * n].rearrange("p (t n) -> p t n", t=KT)).then_inc(prep_hi, 1)

            for i in range(N0):
                prep_take(i)
            with act.Fori(0, PAIRS) as u:
                for j in range(2):
                    act.wait_ge(a_T, 2 * u + j + 1)
                    take(xs[:, j, 0].rearrange("p t n -> p (t n)"), prep_bank[j][:, :]).then_inc(a_hi, 1)
                for j in range(2):
                    b = 2 * u + j
                    act.wait_ge(a_proj, b + 1)
                    hold(act)
                    take(hl[:, bass.ds(b, 1), :], [bQ, bO][j][:, 0:HL].unsqueeze(1)).then_inc(a_hl, 1)
            act.wait_ge(angle_ready, 1)
            nc.scalar.activation(sint, ang, ACT.Sin).then_inc(sin_ready, 1)
            act.wait_ge(cosarg_ready, 1)
            nc.scalar.activation(cost, turns, ACT.Sin).then_inc(cos_ready, 1)
            for i in range(N0, NPREP):
                prep_take(i)
            act.wait_ge(diff_ready, 1)
            nc.scalar.activation(p2, m2, ACT.Exp).then_inc(act_step, 1)
            with act.Fori(0, PAIRS) as u:
                for j in range(2):
                    act.wait_ge(c_T, 2 * u + j + 1)
                    take(hgT[:, j, 0, :], prep_bank[j][:, 0:P]).then_inc(c_hi, 1)
                for j in range(2):
                    act.wait_ge(c_xT, 2 * u + j + 1)
                    take(xs[:, j, 0].rearrange("p t n -> p (t n)"), [bQ, bO][j][:, :]).then_inc(c_xhi, 1)
                for j in range(2):
                    act.wait_ge(c_out[j], 16 * u + 16)

            def k_cache_hi(t, j):
                act.wait_ge(kc_done, 2 * t + j + 3)
                take(kT[:, j, 0, 0:CACHE], bK[:, :]).then_inc(kc_hi, 1)

            def values_cache_hi(t, j):
                act.wait_ge(v_in[j], 16 * CT * (t + 1))
                wait(act, pv_done, 2 * t + j - 1)
                take(vs[:, j, 0, 0:CT, :], vraw[:, j]).then_inc(vc_hi, 1)

            def q_out(t, j):
                n = 2 * t + j + 1
                act.wait_ge(q_done, n + 1)
                wait(act, q_mul, n)
                take(qs, bQ[:, :]).then_inc(q_copied, 1)

            def q_square(t, j):
                n = 2 * t + j + 1
                act.wait_ge(q_copied, n + 1)
                wait(act, q_summed, n)
                nc.scalar.activation(sq, qs, ACT.Square).then_inc(q_squared, 1)

            def kv_out(t, j):
                n, m = 2 * t + j + 1, (j + 1) % 2
                act.wait_ge(kv_done, n + 1)
                wait(act, k_mul, n)
                wait(act, vn_split, n)
                take(ks, bK[:, 0:2 * HD]).then_inc(kv_copied, 1)
                take(vs[:, m, 0, CT, :], bK[:, HD:2 * HD]).then_inc(vn_hi, 1)
                act.wait_ge(kv_copied, n + 1)
                wait(act, rk_ready, n)
                nc.scalar.activation(ksq, ks[:, 0:HD], ACT.Square, accum_out=ssk).then_inc(k_squared, 1)

            def exps(t, j, h):
                g = 2 * t + j
                act.wait_ge(bias_ready, 4 * g + h + 1)
                nc.scalar.activation(pr[:, h, :], pr[:, h, :], ACT.Exp, bias=nbias[:, h:h + 1],
                                     scale=rq[:, j, h:h + 1], accum_out=sums[:, h:h + 1]).then_inc(exp_done, 1)

            def normalise(t, j, h, d=0):
                act.wait_ge(rinv_ready, 4 * (2 * t + j + d) + h + 1)
                nc.scalar.activation(pr[:, h, :], pr[:, h, :], ACT.Copy,
                                     scale=rinv[:, h:h + 1]).then_inc(norm_act, 1)

            def o_hi_out(t, j):
                act.wait_ge(pv_done, 2 * t + j)
                take(ot[:, 0].rearrange("p h n -> p (h n)"), bO[:, :]).then_inc(o_hi, 1)

            def probs_hi(t, j, k, d=0):
                g = 2 * t + j + d
                act.wait_ge(pT_done, UNITS * g + k + 1)
                take(pt[:, 0].rearrange("p h t n -> p (h t n)")[:, k * 512:(k + 1) * 512],
                     bT[(j + d + k) % 2][:, :]).then_inc(p_hi, 1)

            def q_T_hi(t, j):
                n, m = 2 * t + j + 1, (j + 1) % 2
                act.wait_ge(qT_done, n + 1)
                take(qT[:, m, 0].rearrange("p h n -> p (h n)"), bW[:, :]).then_inc(qT_hi, 1)

            def k_new_hi(t, j):
                n, m = 2 * t + j + 1, (j + 1) % 2
                act.wait_ge(kT_done, n + 1)
                take(kT[:, m, 0, CACHE:KEYS], bQ[:, 0:P]).then_inc(kn_hi, 1)

            def wkv_take(t):
                act.wait_ge(kT_done, 2 * t + 2)
                hold(act)
                take(tile_of(wkvT, t, 0), bQ[:, P:3 * P]).then_inc(wkv_hi, 1)

            def w_take(t, j):
                act.wait_ge(woT_done if j else wqT_done, t + 1)
                hold(act)
                take(columns_of(woT if j else wqT, t, 0), bW[:, :].rearrange("p (c n) -> p c n", c=4)).then_inc(
                    wo_hi if j else wq_hi, 1)

            def turn(t):
                for j in range(2):
                    this, nxt, prev, after = (there(t, j, d) for d in (0, 1, -1, 2))
                    if prev:
                        normalise(t, j, 3, -1)
                    if nxt:
                        q_out(t, j)
                    if this:
                        values_cache_hi(t, j)
                    if prev:
                        probs_hi(t, j, 3, -1)
                        probs_hi(t, j, 4, -1)
                    if this:
                        exps(t, j, 0)
                        exps(t, j, 1)
                    if nxt:
                        q_square(t, j)
                    if this:
                        normalise(t, j, 0)
                        exps(t, j, 2)
                    if prev:
                        o_hi_out(t, j)
                    if nxt:
                        kv_out(t, j)
                        q_T_hi(t, j)
                    if this:
                        normalise(t, j, 2)
                        probs_hi(t, j, 0)
                        exps(t, j, 3)
                    if nxt:
                        k_new_hi(t, j)
                        if j == 0 and weights(t):
                            wkv_take(t)
                    if this:
                        probs_hi(t, j, 1)
                    if weights(t):
                        w_take(t, j)
                    if this:
                        probs_hi(t, j, 2)
                    if after:
                        k_cache_hi(t, j)

            turn(-1)
            turn(0)
            with act.Fori(1, TURNS - 1) as t:
                turn(t)
            turn(TURNS - 1)
            turn(TURNS)

        @block.vector
        def _(dve):
            steps = [0]

            def step(ins):
                steps[0] += 1
                ins.then_inc(dve_step, 1)
                dve.wait_ge(dve_step, steps[0])

            def rest(dst, src, hi):
                return nc.vector.tensor_tensor(dst, src, hi.bitcast(FP32), ALU.subtract)

            def prep_rest(i):
                _, n, dst = prep[i]
                dve.wait_ge(prep_hi, i + 1)
                rest(dst[1], prep_bank[i % 2][:, 0:KT * n].rearrange("p (t n) -> p t n", t=KT),
                     dst[0]).then_inc(prep_lo, 1)

            dve.wait_ge(consts_in, 16 * 6)
            dve.wait_ge(const_ready, 1)
            step(nc.vector.tensor_copy(lenf, ints[:, 0:8]))
            nc.vector.tensor_copy(langf, ints[:, 8:16]).then_inc(lens_ready, 1)
            step(nc.vector.tensor_scalar(posf, lenf, tokf, None, ALU.add))
            for q in range(4):
                r = slice(q * PAGE, (q + 1) * PAGE)
                step(nc.vector.tensor_copy(pageidx[r, :, :],
                                           tab[r, :].rearrange("p (b c q) -> p b c q", b=ROWS, q=4)[:, :, :, q]))
                step(nc.vector.tensor_scalar(pageidx[r, :, :], pageidx[r, :, :], 0.0, 63.0, ALU.max, ALU.min))
                step(nc.vector.tensor_scalar(pageidx[r, :, :], pageidx[r, :, :], float(PAGE * KVH),
                                             float(-q * PAGE * KVH), ALU.mult, ALU.add))
            nc.vector.tensor_scalar(pageidx[:, :, :], pageidx[:, :, :], tok8, None, ALU.add).then_inc(idx_step, 1)
            for i in range(N0):
                prep_rest(i)
            half_hd = HD // 2
            for b in range(ROWS):
                last = nc.vector.tensor_scalar(ang[:, b * half_hd:(b + 1) * half_hd], wn[:, 1, 0:half_hd],
                                               posf[:, b:b + 1], None, ALU.mult)
            step(last)
            step(nc.vector.tensor_scalar(turns, ang, 1.0 / TWO_PI, ROUND, ALU.mult, ALU.add))
            step(nc.vector.tensor_scalar(turns, turns, -ROUND, None, ALU.add))
            for c in two_pi_parts():
                step(nc.vector.scalar_tensor_tensor(ang, turns, -c, ang, ALU.mult, ALU.add))
            nc.vector.tensor_scalar(ang, ang, 3.1415925, -3.1415925, ALU.min, ALU.max).then_inc(angle_ready, 1)
            dve.wait_ge(angle_ready, 1)
            step(nc.vector.scalar_tensor_tensor(turns, ang, -1.0, ang, ALU.mult, ALU.max))
            nc.vector.tensor_scalar(turns, turns, -1.0, math.pi / 2, ALU.mult, ALU.add).then_inc(cosarg_ready, 1)
            root = math.sqrt(HD)
            step(nc.vector.tensor_scalar(wn[:, 1, :], wn[:, 0, :], -1.0, None, ALU.mult))
            step(nc.vector.tensor_copy(wn[:, 1, 0:half_hd], wn[:, 0, 0:half_hd]))
            step(nc.vector.tensor_scalar(wn[:, 2, :], wn[:, 2, :], root, None, ALU.mult))
            step(nc.vector.tensor_scalar(wn[:, 3, :], wn[:, 2, :], -1.0, None, ALU.mult))
            nc.vector.tensor_copy(wn[:, 3, 0:half_hd], wn[:, 2, 0:half_hd]).then_inc(wn_ready, 1)

            dve.wait_ge(acc_in, 16)
            with dve.Fori(0, PAIRS) as u:
                for j in range(2):
                    dve.wait_ge(a_hi, 2 * u + j + 1)
                    rest(xs[:, j, 1].rearrange("p t n -> p (t n)"), prep_bank[j][:, :],
                         xs[:, j, 0].rearrange("p t n -> p (t n)")).then_inc(a_lo, 1)
                for j in range(2):
                    row = acc[:, bass.ds(2 * u + j, 1), :]
                    dve.wait_ge(a_proj, 2 * u + j + 1)
                    nc.vector.tensor_tensor(row, bT[j][:, :].unsqueeze(1), row, ALU.add).then_inc(a_add, 1)
            for i in range(N0, NPREP):
                prep_rest(i)

            dve.wait_ge(a_hl, ROWS)
            dve.wait_ge(experts_ready, 1)
            lg, eq, oh1, oh2, rev, num, gates = (gwork[:, i, :] for i in range(7))

            def by_row(v):
                return v.rearrange("p (b e) -> p b e", b=ROWS)

            def wide(v):
                return v.unsqueeze(2).to_broadcast([P, ROWS, EXPERTS])

            def first_largest(onehot, best):
                step(nc.vector.tensor_reduce(best, by_row(lg), AX.X, ALU.max))
                step(nc.vector.tensor_tensor(by_row(eq), by_row(lg), wide(best), ALU.is_equal))
                step(nc.vector.tensor_tensor(eq, eq, rev, ALU.mult))
                step(nc.vector.tensor_reduce(top1, by_row(eq), AX.X, ALU.max))
                step(nc.vector.tensor_tensor(by_row(onehot), by_row(eq), wide(top1), ALU.is_equal))

            step(nc.vector.tensor_tensor(by_row(eq), by_row(num), wide(langf), ALU.is_equal))
            step(nc.vector.scalar_tensor_tensor(by_row(lg), by_row(eq), LANG_BIAS, hl[:, :, ER:HL], ALU.mult, ALU.add))
            first_largest(oh1, m1)
            step(nc.vector.scalar_tensor_tensor(lg, oh1, -3e38, lg, ALU.mult, ALU.add))
            first_largest(oh2, m2)
            nc.vector.tensor_tensor(m2, m2, m1, ALU.subtract).then_inc(diff_ready, 1)
            dve.wait_ge(act_step, 1)
            step(nc.vector.tensor_scalar(p1, p2, 1.0, None, ALU.add))
            step(nc.vector.reciprocal(p1, p1))
            step(nc.vector.tensor_tensor(p2, p2, p1, ALU.mult))
            step(nc.vector.tensor_tensor(by_row(oh1), by_row(oh1), wide(p1), ALU.mult))
            step(nc.vector.tensor_tensor(by_row(oh2), by_row(oh2), wide(p2), ALU.mult))
            step(nc.vector.tensor_tensor(gates, oh1, oh2, ALU.add))
            step(nc.vector.tensor_scalar(gates, gates, LORA_SCALE, None, ALU.mult))
            dve.wait_ge(comp_ready, 4)
            with dve.Fori(0, PAIRS) as u:
                for j in range(2):
                    b = 2 * u + j
                    nc.vector.tensor_tensor(
                        hgb[:, j, :].rearrange("p (e r) -> p e r", e=EXPERTS),
                        hl[:, bass.ds(b, 1), 0:ER].rearrange("p b (e r) -> p (b e) r", e=EXPERTS),
                        gates[:, bass.ds(b * EXPERTS, EXPERTS)].unsqueeze(2).to_broadcast([P, EXPERTS, RANK]),
                        ALU.mult).then_inc(c_hg, 1)
                for j in range(2):
                    dve.wait_ge(c_hi, 2 * u + j + 1)
                    rest(hgT[:, j, 1, :], prep_bank[j][:, 0:P], hgT[:, j, 0, :]).then_inc(c_lo, 1)
                for j in range(2):
                    dve.wait_ge(c_lora, 2 * u + j + 1)
                    row = acc[:, bass.ds(2 * u + j, 1), :].rearrange("p a n -> p (a n)")
                    nc.vector.tensor_tensor(x1[j], bT[j][:, :], row, ALU.add).then_inc(c_x1, 1)
                for j in range(2):
                    dve.wait_ge(c_xhi, 2 * u + j + 1)
                    rest(xs[:, j, 1].rearrange("p t n -> p (t n)"), [bQ, bO][j][:, :],
                         xs[:, j, 0].rearrange("p t n -> p (t n)")).then_inc(c_xlo, 1)
                dve.wait_ge(c_acc, 2 * u + 2)

            def head_max(t, j, h):
                g = 2 * t + j
                dve.wait_ge(scores_done, 4 * g + h + 1)
                if h == 0:
                    dve.wait_ge(mask_ready, g + 1)
                wait(dve, pT_done, UNITS * (g - 1) + h + 2)
                hold(dve)
                nc.vector.tensor_tensor_reduce(out=pr[:, h, :], in0=bS, in1=mask[:, j, :], scale=1.0, scalar=-3e38,
                                               op0=ALU.add, op1=ALU.max,
                                               accum_out=maxs[:, h:h + 1]).then_inc(max_done, 1)
                dve.wait_ge(max_done, 4 * g + h + 1)
                dve.wait_ge(rq_ready, g + 1)
                nc.vector.scalar_tensor_tensor(nbias[:, h:h + 1], maxs[:, h:h + 1], -1.0, rq[:, j, h:h + 1],
                                               ALU.mult, ALU.mult).then_inc(bias_ready, 1)

            def head_sum(t, j, h):
                g = 2 * t + j
                dve.wait_ge(exp_done, 4 * g + h + 1)
                nc.vector.reciprocal(rinv[:, h:h + 1], sums[:, h:h + 1]).then_inc(rinv_ready, 1)

            def normalise(t, j, h):
                dve.wait_ge(rinv_ready, 4 * (2 * t + j) + h + 1)
                nc.vector.tensor_scalar(pr[:, h, :], pr[:, h, :], rinv[:, h:h + 1], None,
                                        ALU.mult).then_inc(norm_dve, 1)

            def q_add(t, j):
                n, half_hd = 2 * t + j + 1, HD // 2
                a3, b3, r3 = (v.rearrange("p (h n) -> p h n", h=REP) for v in (u1, u2, qr))
                dve.wait_ge(q_mul, n + 1)
                wait(dve, qT_done, n)
                nc.vector.tensor_tensor(r3[:, :, 0:half_hd], a3[:, :, 0:half_hd], b3[:, :, half_hd:HD], ALU.add)
                nc.vector.tensor_tensor(r3[:, :, half_hd:HD], a3[:, :, half_hd:HD], b3[:, :, 0:half_hd],
                                        ALU.add).then_inc(qr_ready, 1)

            def k_cache_lo(t, j):
                n, m = 2 * t + j + 1, (j + 1) % 2
                dve.wait_ge(kc_hi, n + 1)
                rest(kT[:, m, 1, 0:CACHE], bK[:, :], kT[:, m, 0, 0:CACHE]).then_inc(kc_lo, 1)

            def make_mask(t, j):
                n, m, uses = 2 * t + j + 1, (j + 1) % 2, t + 1 + j
                dve.wait_ge(rope_in[m], 16 * uses)
                nc.vector.tensor_scalar(mask[:, m, 0:CACHE], keyno[:, :], rope[:, m, 4 * HD:4 * HD + 1], NEG,
                                        ALU.is_ge, ALU.mult).then_inc(mask_ready, 1)

            def values_cache_lo(t, j):
                dve.wait_ge(vc_hi, 2 * t + j + 1)
                rest(vs[:, j, 1, 0:CT, :], vraw[:, j], vs[:, j, 0, 0:CT, :]).then_inc(vc_split, 1)

            def q_sum(t, j):
                n, m = 2 * t + j + 1, (j + 1) % 2
                dve.wait_ge(q_squared, n + 1)
                nc.vector.tensor_reduce(ssq[:, m, :], sq.rearrange("p (h n) -> p h n", h=REP), AX.X,
                                        ALU.add).then_inc(q_summed, 1)

            def o_lo_out(t, j):
                dve.wait_ge(o_hi, 2 * t + j)
                rest(ot[:, 1].rearrange("p h n -> p (h n)"), bO[:, :],
                     ot[:, 0].rearrange("p h n -> p (h n)")).then_inc(o_lo, 1)

            def probs_lo(t, j, k, d=0):
                g = 2 * t + j + d
                dve.wait_ge(p_hi, UNITS * g + k + 1)
                c = slice(k * 512, (k + 1) * 512)
                rest(pt[:, 1].rearrange("p h t n -> p (h t n)")[:, c], bT[(j + d + k) % 2][:, :],
                     pt[:, 0].rearrange("p h t n -> p (h t n)")[:, c]).then_inc(p_lo, 1)

            def k_rope(t, j):
                n, m = 2 * t + j + 1, (j + 1) % 2
                dve.wait_ge(rk_ready, n + 1)
                wait(dve, kT_done, n)
                nc.vector.scalar_tensor_tensor(kr1, ks[:, 0:HD], rk, rope[:, m, 2 * HD:3 * HD], ALU.mult, ALU.mult)
                nc.vector.scalar_tensor_tensor(kr2, ks[:, 0:HD], rk, rope[:, m, 3 * HD:4 * HD], ALU.mult,
                                               ALU.mult).then_inc(k_mul, 1)
                dve.wait_ge(k_mul, n + 1)
                h = HD // 2
                nc.vector.tensor_tensor(kr[:, 0:h], kr1[:, 0:h], kr2[:, h:HD], ALU.add)
                nc.vector.tensor_tensor(kr[:, h:HD], kr1[:, h:HD], kr2[:, 0:h], ALU.add).then_inc(kr_ready, 1)

            def q_T_lo(t, j):
                n, m = 2 * t + j + 1, (j + 1) % 2
                dve.wait_ge(qT_hi, n + 1)
                rest(qT[:, m, 1].rearrange("p h n -> p (h n)"), bW[:, :],
                     qT[:, m, 0].rearrange("p h n -> p (h n)")).then_inc(qT_lo, 1)

            def add_out(t, j):
                f = 2 * t + j - 1
                dve.wait_ge(wo_done, f + 1)
                row = acc[:, at(f % ROWS), :].rearrange("p a n -> p (a n)")
                nc.vector.tensor_tensor(row, bO[:, :], row, ALU.add).then_inc(added, 1)

            def k_new_lo(t, j):
                n, m = 2 * t + j + 1, (j + 1) % 2
                dve.wait_ge(kn_hi, n + 1)
                if j == 0 and weights(t):
                    dve.wait_ge(wkv_hi, t + 1)
                rest(kT[:, m, 1, CACHE:KEYS], bQ[:, 0:P], kT[:, m, 0, CACHE:KEYS]).then_inc(kn_lo, 1)

            def wkv_rest(t):
                dve.wait_ge(wkv_hi, t + 1)
                rest(tile_of(wkvT, t, 1), bQ[:, P:3 * P], tile_of(wkvT, t, 0)).then_inc(wkv_lo, 1)

            def w_rest(t, j):
                dve.wait_ge(wo_hi if j else wq_hi, t + 1)
                w = woT if j else wqT
                rest(columns_of(w, t, 1), bW[:, :].rearrange("p (c n) -> p c n", c=4),
                     columns_of(w, t, 0)).then_inc(wo_lo if j else wq_lo, 1)

            def turn(t):
                for j in range(2):
                    this, nxt, prev = (there(t, j, d) for d in (0, 1, -1))
                    if this:
                        head_max(t, j, 0)
                    if prev:
                        probs_lo(t, j, 2, -1)
                    if nxt:
                        k_cache_lo(t, j)
                    if this:
                        head_max(t, j, 1)
                    if prev:
                        probs_lo(t, j, 3, -1)
                        probs_lo(t, j, 4, -1)
                    if nxt:
                        make_mask(t, j)
                    if this:
                        head_max(t, j, 2)
                        head_sum(t, j, 0)
                        values_cache_lo(t, j)
                        head_sum(t, j, 1)
                    if nxt:
                        q_add(t, j)
                        q_sum(t, j)
                    if this:
                        normalise(t, j, 1)
                    if prev:
                        o_lo_out(t, j)
                    if this:
                        head_sum(t, j, 2)
                        head_max(t, j, 3)
                    if nxt:
                        k_rope(t, j)
                        q_T_lo(t, j)
                    if this:
                        probs_lo(t, j, 0)
                    if nxt:
                        k_new_lo(t, j)
                        if j == 0 and weights(t):
                            wkv_rest(t)
                    if this:
                        head_sum(t, j, 3)
                    if prev:
                        add_out(t, j)
                    if this:
                        probs_lo(t, j, 1)
                    if weights(t):
                        w_rest(t, j)

            dve.wait_ge(pool_step, 2)
            turn(-1)
            turn(0)
            with dve.Fori(1, TURNS - 1) as t:
                turn(t)
            turn(TURNS - 1)
            turn(TURNS)

        @block.gpsimd
        def _(pool):
            key_rows = kc.rearrange("g s h d -> (g s h) d")
            value_rows = vc.rearrange("g s h d -> (g s h) d")
            nc.gpsimd.iota(tok8, [[0, 1]], base=0, channel_multiplier=KVH, allow_small_or_imprecise_dtypes=True)
            nc.gpsimd.iota(tokf, [[0, 1]], base=0, channel_multiplier=1,
                           allow_small_or_imprecise_dtypes=True).then_inc(const_ready, 1)
            nc.gpsimd.memset(ident[:, :], 0.0).then_inc(pool_step, 1)
            pool.wait_ge(pool_step, 1)
            nc.gpsimd.affine_select(out=ident[:, :], in_=ident[:, :], compare_op=ALU.not_equal, fill=1.0, base=0,
                                    pattern=[[-1, P]], channel_multiplier=1).then_inc(ident_ready, 1)
            nc.gpsimd.memset(half, -0.5)
            nc.gpsimd.memset(one4, 1.0)
            nc.gpsimd.memset(mask[:, :, CACHE:KEYS], 0.0)
            rev, num = gwork[:, 4, :], gwork[:, 5, :]
            nc.gpsimd.iota(rev, [[0, ROWS], [-1, EXPERTS]], base=EXPERTS, channel_multiplier=0,
                           allow_small_or_imprecise_dtypes=True)
            nc.gpsimd.iota(num, [[0, ROWS], [1, EXPERTS]], base=0, channel_multiplier=0,
                           allow_small_or_imprecise_dtypes=True).then_inc(experts_ready, 1)
            pool.wait_ge(wn_ready, 1)
            pool.wait_ge(sin_ready, 1)
            pool.wait_ge(cos_ready, 1)
            h = HD // 2
            for i in range(4):
                if i >= 2:
                    pool.wait_ge(comp_out[i % 2], 16)
                wave = (cost, sint)[i % 2].rearrange("p (b n) -> p b n", b=ROWS)
                weight = wn[:, (0, 1, 2, 3)[i], :]
                for s in range(2):
                    last = nc.gpsimd.tensor_tensor(
                        comp[i % 2][:, :, s * h:(s + 1) * h], wave,
                        weight[:, s * h:(s + 1) * h].unsqueeze(1).to_broadcast([P, ROWS, h]), ALU.mult)
                last.then_inc(comp_ready, 1)
            pool.wait_ge(comp_ready, 4)
            nc.gpsimd.iota(keyno[:, :], [[1, CACHE]], base=0, channel_multiplier=0,
                           allow_small_or_imprecise_dtypes=True).then_inc(pool_step, 1)
            with pool.Fori(0, PAIRS) as u:
                for j in range(2):
                    pool.wait_ge(c_x1, 2 * u + j + 1)
                    hold(pool)
                    nc.gpsimd.tensor_copy(acc[:, bass.ds(2 * u + j, 1), :], x1[j].unsqueeze(1)).then_inc(c_acc, 1)

            def gather_keys(b, j, k):
                gk = 2 * k + j
                pool_row = pageidx[:, at(b), :].rearrange("p a c -> p (a c)")
                wait(pool, idx_step, 1 + 2 * gk)
                wait(pool, kc_done, gk - 1)
                hold(pool)
                nc.gpsimd.tensor_copy(kidx[:, j, :], pool_row).then_inc(idx_step, 1)
                wait(pool, idx_step, 2 + 2 * gk)
                hold(pool)
                nc.gpsimd.tensor_tensor(pool_row, pool_row, one4, ALU.add).then_inc(idx_step, 1)
                for c in range(CT):
                    nc.gpsimd.indirect_dma_start(
                        kraw[:, j, c, :], None, key_rows,
                        bass.IndirectOffsetOnAxis(ap=kidx[:, j, c:c + 1], axis=0)).then_inc(k_in[j], 16)

            def gather_values(t, j):
                if there(t, j, 0):
                    pool.wait_ge(vc_split, 2 * t + j + 1)
                    hold(pool)
                for c in range(CT):
                    nc.gpsimd.indirect_dma_start(
                        vraw[:, j, c, :], None, value_rows,
                        bass.IndirectOffsetOnAxis(ap=kidx[:, j, c:c + 1], axis=0)).then_inc(v_in[j], 16)

            def q_tables(t, j):
                n, m, uses = 2 * t + j + 1, (j + 1) % 2, t + 1 + j
                q3, a3, b3 = (v.rearrange("p (h n) -> p h n", h=REP) for v in (qs, u1, u2))
                pool.wait_ge(rope_in[m], 16 * uses)
                pool.wait_ge(q_copied, n + 1)
                wait(pool, qr_ready, n)
                hold(pool)
                nc.gpsimd.tensor_tensor(a3, q3, rope[:, m, 0:HD].unsqueeze(1).to_broadcast([P, REP, HD]), ALU.mult)
                nc.gpsimd.tensor_tensor(b3, q3, rope[:, m, HD:2 * HD].unsqueeze(1).to_broadcast([P, REP, HD]),
                                        ALU.mult).then_inc(q_mul, 1)

            def q_scale(t, j):
                n, m = 2 * t + j + 1, (j + 1) % 2
                pool.wait_ge(q_summed, n + 1)
                hold(pool)
                nc.gpsimd.tensor_scalar(ssq[:, m, :], ssq[:, m, :], HD * EPS, None, ALU.add).then_inc(rq_arg, 1)
                pool.wait_ge(rq_arg, n + 1)
                nc.gpsimd.tensor_tensor(rq[:, m, :], ssq[:, m, :], half, ALU.pow).then_inc(rq_ready, 1)

            def values_new_lo(t, j):
                pool.wait_ge(vn_hi, 2 * t + j + 1)
                nc.gpsimd.tensor_tensor(vs[:, j, 1, CT, :], ks[:, HD:2 * HD], vs[:, j, 0, CT, :].bitcast(FP32),
                                        ALU.subtract).then_inc(vn_split, 1)

            def k_scale(t, j):
                n = 2 * t + j + 1
                pool.wait_ge(k_squared, n + 1)
                wait(pool, k_mul, n)
                hold(pool)
                nc.gpsimd.tensor_scalar(ssk1, ssk, HD * EPS, None, ALU.add).then_inc(rk_arg, 1)
                pool.wait_ge(rk_arg, n + 1)
                nc.gpsimd.tensor_tensor(rk, ssk1, half[:, 0:1], ALU.pow).then_inc(rk_ready, 1)

            def turn(t):
                for j in range(2):
                    this, nxt, after = (there(t, j, d) for d in (0, 1, 2))
                    if this:
                        values_new_lo(t, j)
                    if nxt:
                        q_tables(t, j)
                    if after:
                        gather_keys(((t + 1) % PAIRS) * 2 + j, j, t + 1)
                    if nxt:
                        k_scale(t, j)
                        q_scale(t, j)
                    if after:
                        gather_values(t, j)

            pool.wait_ge(pool_step, 2)
            pool.wait_ge(prep_T, NPREP)
            turn(-1)
            turn(0)
            with pool.Fori(1, TURNS - 1) as t:
                turn(t)
            turn(TURNS - 1)


INPUTS = ["x", "itok_B_0_7", "itok_Bx16_0_63", "itok_B_207_1644", "L0_cond_W", "L0_cond_Wr", "L0_cond_A", "L0_cond_B",
          "L1_cond_Wq", "L1_cond_Wk", "L1_cond_Wv", "L1_cond_Wo", "L1_cond_q_norm_w", "L1_cond_k_norm_w",
          "L1_cond_k_cache", "L1_cond_v_cache"]


def kernel(**inputs):
    import concourse.bacc as bacc
    from concourse.bass_utils import run_bass_kernel_spmd

    nc = bacc.Bacc("TRN2", target_bir_lowering=False, num_devices=1)
    arrays, args = {}, []
    for name in INPUTS:
        a = np.ascontiguousarray(inputs[name])
        arrays[f"in_{name}"] = a
        args.append(nc.dram_tensor(f"in_{name}", a.shape, mybir.dt.from_np(a.dtype), kind="ExternalInput").ap())
    inv = (1.0 / 10000.0 ** (np.arange(0, HD, 2, dtype=np.float64) / HD)).astype(np.float32)
    arrays["inv_freq"] = inv
    args.append(nc.dram_tensor("inv_freq", inv.shape, FP32, kind="ExternalInput").ap())
    out = nc.dram_tensor("out", (ROWS, P, DM), FP32, kind="ExternalOutput").ap()
    build(nc, *args, out)
    return run_bass_kernel_spmd(nc, [arrays], core_ids=[0]).results[0]["out"]
```

```python
import math
from contextlib import ExitStack

import concourse.bass as bass
import numpy as np
from concourse import mybir

FP32 = mybir.dt.float32
FP32R = mybir.dt.float32r
I32 = mybir.dt.int32
U32 = mybir.dt.uint32
ALU = mybir.AluOpType
ACT = mybir.ActivationFunctionType
AX = mybir.AxisListType

P = 128
ROWS, DM = 8, 512
KT = DM // P
EXPERTS, RANK = 8, 16
ER = EXPERTS * RANK
HD = 128
KVH, REP = 8, 4
QW = REP * HD
PAGE, NPP = 32, 16
CACHE = PAGE * NPP
KEYS = CACHE + P
TILES = KEYS // P
CT = CACHE // P
GROUPS = KVH * ROWS
TURNS = GROUPS // 2
PAIRS = ROWS // 2
STEPS = (KVH - 1) * PAIRS
UNITS = REP * TILES // 4
CTX = 4 * HD + 8
HL = ER + EXPERTS
EPS = 1e-6
NEG = -1e30
LANG_BIAS = 5.0
LORA_SCALE = 2.0
TWO_PI = 2 * math.pi
ROUND = 1.5 * 2.0 ** 23


def two_pi_parts():
    a = round(TWO_PI * 64) / 64
    b = round((TWO_PI - a) * 2 ** 17) / 2 ** 17
    return a, b, TWO_PI - a - b


def build(nc, x, lang, table, lens, w0, wr, la, lb, wq, wk, wv, wo, qn, kn, kc, vc, invf, out):
    ctx = ExitStack()
    with ctx:
        def sb(name, shape, dt=FP32):
            return ctx.enter_context(nc.sbuf_tensor(name, shape, dt))

        def ps(name, shape):
            return ctx.enter_context(nc.psum_tensor(name, shape, FP32))

        def sem(name):
            return ctx.enter_context(nc.semaphore(name))

        wqT = sb("wqT", [P, 2, 2, KT, QW], FP32R)
        wkvT = sb("wkvT", [P, 2, 2, KT, 2 * HD], FP32R)
        woT = sb("woT", [P, 2, 2, REP, DM], FP32R)
        xs = sb("xs", [P, 2, 2, KT, P], FP32R)
        rope = sb("rope", [P, 2, CTX])
        kraw = sb("kraw", [P, 2, CT, HD])
        vraw = sb("vraw", [P, 2, CT, HD])
        kT = sb("kT", [P, 2, 2, KEYS], FP32R)
        vs = sb("vs", [P, 2, 2, TILES, HD], FP32R)
        qT = sb("qT", [P, 2, 2, REP, P], FP32R)
        pr = sb("pr", [P, REP, KEYS])
        pt = sb("pt", [P, 2, REP, TILES, P], FP32R)
        ot = sb("ot", [P, 2, REP, P], FP32R)
        mask = sb("mask", [P, 2, KEYS])
        qwork = sb("qwork", [P, 5, QW])
        kwork = sb("kwork", [P, 6, HD])
        wraw = sb("wraw", [P, 2, QW + 2 * HD])
        acc = sb("acc", [P, ROWS, DM])
        ident = sb("ident", [P, P])
        keyno = sb("keyno", [P, CACHE])
        pageidx = sb("pageidx", [P, ROWS, CT])
        kidx = sb("kidx", [P, 2, CT], U32)
        tab = sb("tab", [P, ROWS * NPP], I32)
        small = sb("small", [P, 128])
        qs, sq, u1, u2, qr = (qwork[:, i, :] for i in range(5))
        ks = kwork[:, 0:2, :].rearrange("p a n -> p (a n)")
        kr1, kr2, kr, ksq = (kwork[:, i, :] for i in range(2, 6))
        maxs, nbias, sums, rinv = (small[:, 4 * i:4 * i + 4] for i in range(4))
        ssq = small[:, 16:24].rearrange("p (j h) -> p j h", j=2)
        rq = small[:, 24:32].rearrange("p (j h) -> p j h", j=2)
        ssk, rk, half = small[:, 32:33], small[:, 33:34], small[:, 36:40]
        ssk1 = small[:, 34:35]
        one4 = small[:, 40:44]
        tok8 = small[:, 44:45]
        tokf = small[:, 45:46]
        lenf = small[:, 48:56]
        langf = small[:, 56:64]
        ints = small[:, 64:80].bitcast(I32)
        posf = small[:, 80:88]
        m1, m2, top1, p1, p2 = (small[:, 88 + 8 * i:96 + 8 * i] for i in range(5))
        w0T = wqT[:, 1]
        raT = wkvT[:, 1].rearrange("p a t n -> p (a t n)")[:, 0:2 * KT * HL].rearrange(
            "p (a t n) -> p a t n", a=2, t=KT)
        lbT = woT[:, 1, :, 0, :]
        hgT = [woT[:, 1, :, 1 + i, :] for i in range(2)]
        hl = pr[:, 2:4, :].rearrange("p j n -> p (j n)")[:, 0:ROWS * HL].rearrange("p (b n) -> p b n", b=ROWS)
        gwork = mask[:, 1, 0:7 * ROWS * EXPERTS].rearrange("p (a n) -> p a n", n=ROWS * EXPERTS)
        ang, turns, sint, cost = (qwork[:, i, :] for i in range(4))
        comp = [pr[:, 0, 0:ROWS * HD // 2].rearrange("p (b n) -> p b n", b=ROWS),
                pr[:, 1, 0:ROWS * HD // 2].rearrange("p (b n) -> p b n", b=ROWS)]
        x1_parts = pt[:, :, :, :, :].rearrange("p a h t n -> p (a h t n)")
        wn = keyno[:, :].rearrange("p (a n) -> p a n", a=4)
        hgb = sb("hgb", [P, ROWS // 2, P])

        xT_d = nc.dram_tensor("xT_scratch", (ROWS, P, 2 * KT * P), FP32, kind="Internal").ap()
        rope_d = nc.dram_tensor("rope_scratch", (ROWS, P, CTX), FP32, kind="Internal").ap()

        two_banks = ps("two_banks", [P, 1024])
        bS = two_banks[:, :].rearrange("p (a n) -> p a n", a=2)[:, :, 0:KEYS // 2]
        halves = [two_banks[:, 0:512], two_banks[:, 512:1024]]
        bT = [ps("bT0", [P, 512]), ps("bT1", [P, 512])]
        bQ, bK, bO, bW = (ps(n, [P, 512]) for n in ("bQ", "bK", "bO", "bW"))

        scores_done, kc_done, q_done, kv_done = (sem(n) for n in ("scores_done", "kc_done", "q_done", "kv_done"))
        qT_done, kT_done, pT_done, pv_done, wo_done = (
            sem(n) for n in ("qT_done", "kT_done", "pT_done", "pv_done", "wo_done"))
        wqT_done, woT_done = sem("wqT_done"), sem("woT_done")
        kc_hi, kc_lo, kn_hi, kn_lo, qT_hi, qT_lo = (
            sem(n) for n in ("kc_hi", "kc_lo", "kn_hi", "kn_lo", "qT_hi", "qT_lo"))
        p_hi, p_lo, o_hi, o_lo = (sem(n) for n in ("p_hi", "p_lo", "o_hi", "o_lo"))
        wq_hi, wq_lo, wkv_hi, wkv_lo, wo_hi, wo_lo = (
            sem(n) for n in ("wq_hi", "wq_lo", "wkv_hi", "wkv_lo", "wo_hi", "wo_lo"))
        q_copied, q_squared, q_summed, rq_ready, qr_ready = (
            sem(n) for n in ("q_copied", "q_squared", "q_summed", "rq_ready", "qr_ready"))
        kv_copied, k_squared, rk_ready, kr_ready = (
            sem(n) for n in ("kv_copied", "k_squared", "rk_ready", "kr_ready"))
        max_done, bias_ready, exp_done, rinv_ready, normalised = (
            sem(n) for n in ("max_done", "bias_ready", "exp_done", "rinv_ready", "normalised"))
        mask_ready, vc_split, vn_split, added = (sem(n) for n in ("mask_ready", "vc_split", "vn_split", "added"))
        x_in, rope_in, k_in, v_in, w_in = ([sem(f"{n}{j}") for j in range(2)] for n in
                                           ("x_in", "rope_in", "k_in", "v_in", "w_in"))
        held = sem("held")
        dve_step, pool_step, act_step = sem("dve_step"), sem("pool_step"), sem("act_step")
        rq_arg, rk_arg, q_mul, k_mul, vc_hi, vn_hi = (
            sem(n) for n in ("rq_arg", "rk_arg", "q_mul", "k_mul", "vc_hi", "vn_hi"))
        lens_ready = sem("lens_ready")
        consts_in, ident_ready, const_ready = sem("consts_in"), sem("ident_ready"), sem("const_ready")
        idx_step = sem("idx_step")
        prep_in = [sem(f"prep_in{i}") for i in range(6)]
        prep_T, prep_hi, prep_lo = sem("prep_T"), sem("prep_hi"), sem("prep_lo")
        row_in = [sem(f"row_in{b}") for b in range(ROWS)]
        a_T, a_hi, a_lo, a_proj, a_hl, a_add = (sem(n) for n in ("a_T", "a_hi", "a_lo", "a_proj", "a_hl", "a_add"))
        experts_ready, diff_ready, wn_ready = sem("experts_ready"), sem("diff_ready"), sem("wn_ready")
        c_hg, c_T, c_hi, c_lo, c_lora, c_x1, c_xT, c_xhi, c_xlo = (
            sem(n) for n in ("c_hg", "c_T", "c_hi", "c_lo", "c_lora", "c_x1", "c_xT", "c_xhi", "c_xlo"))
        c_out = [sem(f"c_out{i}") for i in range(6)]
        angle_ready, sin_ready, cosarg_ready, cos_ready = (
            sem(n) for n in ("angle_ready", "sin_ready", "cosarg_ready", "cos_ready"))
        comp_ready, comp_out, lens_out = sem("comp_ready"), [sem("comp_out0"), sem("comp_out1")], sem("lens_out")
        out_stored = sem("out_stored")

        def wait(eng, s, n):
            if not isinstance(n, int) or n > 0:
                eng.wait_ge(s, n)

        def hold(eng):
            eng.sem_inc(held, 1)

        prep = []
        for o in range(KT):
            prep.append((w0[o * P:(o + 1) * P, :], P, [w0T[:, a, :, o * P:(o + 1) * P] for a in range(2)]))
        prep.append((la.rearrange("e r d -> (e r) d"), P, [raT[:, a, :, 0:ER] for a in range(2)]))
        prep.append((wr, EXPERTS, [raT[:, a, :, ER:HL] for a in range(2)]))
        N0 = len(prep)
        for e in range(REP):
            prep.append((wq[e * P:(e + 1) * P, :], P, [wqT[:, 0, a, :, e * P:(e + 1) * P] for a in range(2)]))
        prep.append((wk[0:HD, :], P, [wkvT[:, 0, a, :, 0:HD] for a in range(2)]))
        prep.append((wv[0:HD, :], P, [wkvT[:, 0, a, :, HD:2 * HD] for a in range(2)]))
        prep.append((None, P, [lbT[:, a, :].rearrange("p (t n) -> p t n", t=KT) for a in range(2)]))
        for o in range(KT):
            prep.append((wo[o * P:(o + 1) * P, 0:QW], P, [woT[:, 0, a, :, o * P:(o + 1) * P] for a in range(2)]))
        NPREP = len(prep)
        last_staged = [max(i for i in range(NPREP) if i % 6 == k) + 1 for k in range(6)]
        loads = [EXPERTS if w[0] is None else 1 for w in prep]
        prep_count = [16 * sum(loads[i % 6:i + 1:6]) for i in range(NPREP)]
        beside_row = [range(N0 + 2 * b, min(N0 + 2 * b + 2, NPREP)) for b in range(ROWS)]
        stage = [kraw[:, 0].rearrange("p t n -> p (t n)"), kraw[:, 1].rearrange("p t n -> p (t n)"),
                 vraw[:, 0].rearrange("p t n -> p (t n)"), vraw[:, 1].rearrange("p t n -> p (t n)"),
                 wraw[:, 0, 0:QW], wraw[:, 1, 0:QW]]
        x_bank = [bW, bK]
        gated_bank = [halves[0], bO[:, :]]

        def x1_place(b):
            if b < 2:
                return xs[:, b].rearrange("p a t n -> p (a t n)")
            k = (b - 2) % 4
            return x1_parts[:, 2 * k * DM:2 * (k + 1) * DM]

        def x1_slot(b):
            return (b, 0) if b < 2 else (2 + (b - 2) % 4, 16 * ((b - 2) // 4))

        def at(i, n=1):
            return slice(i * n, (i + 1) * n) if isinstance(i, int) else bass.ds(i * n, n)

        def part_of(view, kv, a, tile):
            return view[:, at(kv % 2), a, tile, :].rearrange("p k n -> p (k n)")

        def columns_of(view, s, a):
            return view[:, at((s // PAIRS + 1) % 2), a, :, at(s % PAIRS, P)].rearrange("p k t n -> p (k t) n")

        def tile_of(view, s, a):
            return view[:, at((s // PAIRS + 1) % 2), a, at(s % PAIRS), :].rearrange("p k t n -> p (k t n)")

        def there(t, j, d):
            return not isinstance(t, int) or 0 <= 2 * t + j + d < GROUPS

        def step_of(t, j, on):
            s = t + j
            return s if on and (not isinstance(t, int) or 0 <= s < STEPS) else None

        def kv_of_next(t, j):
            return t // PAIRS if j == 0 else (t + 1) // PAIRS

        def kv_of_last(t, j):
            return (t - 1) // PAIRS if j == 0 else t // PAIRS

        block = ctx.enter_context(nc.Block())

        @block.sync
        def _(sp):
            def load_consts():
                sp.dma_start(tab[:, :], table.rearrange("b n -> (b n)").partition_broadcast(P)).then_inc(consts_in, 16)
                sp.dma_start(ints[:, 0:8], lens.partition_broadcast(P)).then_inc(consts_in, 16)
                sp.dma_start(ints[:, 8:16], lang.partition_broadcast(P)).then_inc(consts_in, 16)
                sp.dma_start(wn[:, 0, :], qn.partition_broadcast(P)).then_inc(consts_in, 16)
                sp.dma_start(wn[:, 2, :], kn.partition_broadcast(P)).then_inc(consts_in, 16)
                sp.dma_start(sint[:, 0:HD // 2], invf.partition_broadcast(P)).then_inc(consts_in, 16)

            def load_weight(i):
                src, n, _ = prep[i]
                if i >= 6:
                    sp.wait_ge(prep_T, i - 5)
                dst = stage[i % 6]
                if src is None:
                    for e in range(EXPERTS):
                        d = dst.rearrange("p (t e r) -> p t e r", t=KT, e=EXPERTS)[:, :, e, :]
                        sp.dma_start(d, lb[e].rearrange("(t p) r -> p t r", p=P)).then_inc(prep_in[i % 6], 16)
                else:
                    sp.dma_start(dst[0:n, :], src).then_inc(prep_in[i % 6], 16)

            def load_row(b):
                sp.dma_start(acc[:, b, :], x[b]).then_inc(row_in[b], 16)

            load_row(0)
            for i in range(KT):
                load_weight(i)
            load_row(1)
            for i in range(KT, N0):
                load_weight(i)
            load_row(2)
            load_consts()
            for b in range(3, ROWS):
                load_row(b)
            for i in range(N0, NPREP):
                load_weight(i)

            half_hd = HD // 2
            for i in range(8):
                sp.wait_ge(comp_ready, i + 1)
                sp.dma_start(rope_d[:, :, i * half_hd:(i + 1) * half_hd].rearrange("b p n -> p b n"),
                             comp[i % 2]).then_inc(comp_out[i % 2], 16)
            sp.wait_ge(lens_ready, 1)
            sp.dma_start(rope_d[:, :, 4 * HD:4 * HD + 1].rearrange("b p n -> p b n"),
                         lenf.unsqueeze(2), allow_slow_non_contiguous=True).then_inc(lens_out, 16)
            sp.wait_ge(comp_out[0], 64)
            sp.wait_ge(comp_out[1], 64)
            sp.wait_ge(lens_out, 16)

            def load_tables(b, j):
                sp.dma_start(rope[:, j, 0:4 * HD + 1],
                             rope_d[at(b), :, 0:4 * HD + 1].rearrange("a p n -> p (a n)")).then_inc(rope_in[j], 16)

            def load_group(b, j):
                sp.dma_start(xs[:, j].rearrange("p a t n -> p (a t n)").bitcast(FP32),
                             xT_d[at(b)].rearrange("a p n -> p (a n)")).then_inc(x_in[j], 16)
                load_tables(b, j)

            def load_weights(i, s):
                kv, part = s // PAIRS + 1, s % PAIRS
                if i == 0:
                    sp.dma_start(wraw[:, 0, 0:QW], wq[at(kv * REP + part, P), :]).then_inc(w_in[0], 16)
                    sp.dma_start(wraw[:, 0, QW:QW + HD], wk[at(kv, HD), at(part, P)]).then_inc(w_in[0], 16)
                    sp.dma_start(wraw[:, 0, QW + HD:QW + 2 * HD], wv[at(kv, HD), at(part, P)]).then_inc(w_in[0], 16)
                else:
                    sp.dma_start(wraw[:, 1, 0:QW], wo[at(part, P), at(kv, QW)]).then_inc(w_in[1], 16)

            def turn(t, weights, store):
                for j in range(2):
                    g = 2 * t + j
                    wait(sp, kv_done, g + 1)
                    wait(sp, q_mul, g + 1)
                    wait(sp, k_mul, g + 1)
                    wait(sp, mask_ready, g + 1)
                    load_group(((t + 1) % PAIRS) * 2 + j, j)
                    if weights:
                        if j == 0:
                            sp.wait_ge(wqT_done, t + 1)
                            sp.wait_ge(kv_done, 2 * t + 1)
                        else:
                            sp.wait_ge(woT_done, t + 1)
                        load_weights(j, t + 1)
                    if store:
                        store_row(g - 2)

            def store_row(g):
                sp.wait_ge(added, g + 1)
                b = g % ROWS
                sp.dma_start(out[at(b)].rearrange("a p n -> p (a n)"),
                             acc[:, at(b), :].rearrange("p a n -> p (a n)")).then_inc(out_stored, 16)

            load_tables(0, 0)
            load_tables(1, 1)
            sp.wait_ge(prep_T, NPREP)
            load_weights(0, 0)
            load_weights(1, 0)
            for b in range(ROWS):
                sp.wait_ge(c_xlo, b + 1)
                sp.dma_start(xT_d[b], x1_place(b).bitcast(FP32)).then_inc(c_out[x1_slot(b)[0]], 16)
            for b in range(2, ROWS):
                sp.wait_ge(c_out[x1_slot(b)[0]], x1_slot(b)[1] + 16)
            sp.wait_ge(c_out[0], 16)
            sp.wait_ge(c_out[1], 16)
            turn(0, True, False)
            with sp.Fori(1, STEPS - 1) as t:
                turn(t, True, False)
            with sp.Fori(STEPS - 1, TURNS - 3) as t:
                turn(t, False, False)
            with sp.Fori(TURNS - 3, TURNS - 1) as t:
                turn(t, False, True)
            for g in range(GROUPS - 4, GROUPS):
                store_row(g)
            sp.wait_ge(out_stored, 16 * ROWS)

        @block.tensor
        def _(pe):
            def mm3(dst, lhs, rhs, first, last):
                nc.tensor.matmul(dst, lhs[0], rhs[0], start=first, stop=False)
                nc.tensor.matmul(dst, lhs[0], rhs[1], start=False, stop=False)
                return nc.tensor.matmul(dst, lhs[1], rhs[0], start=False, stop=last)

            pe.wait_ge(ident_ready, 1)

            def prep_unit(i):
                _, n, _ = prep[i]
                pe.wait_ge(prep_in[i % 6], prep_count[i])
                if i >= 2:
                    pe.wait_ge(prep_lo, i - 1)
                for c in range(KT):
                    src = stage[i % 6][0:n, c * P:(c + 1) * P]
                    last = nc.tensor.transpose(halves[i % 2][:, c * n:(c + 1) * n], src, ident[0:n, 0:n])
                last.then_inc(prep_T, 1)

            def x_T(b):
                pe.wait_ge(row_in[b], 16)
                for c in range(KT):
                    last = nc.tensor.transpose(x_bank[b % 2][:, c * P:(c + 1) * P], acc[:, b, c * P:(c + 1) * P],
                                               ident[:, :])
                last.then_inc(a_T, 1)

            def x_products(b):
                j = b % 2
                pe.wait_ge(a_lo, b + 1)
                if b == 0:
                    pe.wait_ge(prep_lo, N0)
                wait(pe, a_add, b - 1)
                wait(pe, a_hl, b - 1)
                for c in range(KT):
                    mm3(bT[j][:, :], [xs[:, j, a, c, :] for a in range(2)],
                        [w0T[:, a, c, :] for a in range(2)], c == 0, c == KT - 1)
                for c in range(KT):
                    last = mm3([bQ, bO][j][:, 0:HL], [xs[:, j, a, c, :] for a in range(2)],
                               [raT[:, a, c, :] for a in range(2)], c == 0, c == KT - 1)
                last.then_inc(a_proj, 1)

            def gated_T(i):
                pe.wait_ge(c_hg, i + 1)
                if i == 0:
                    pe.wait_ge(prep_lo, NPREP)
                else:
                    pe.wait_ge(a_hl, ROWS)
                for b in range(ROWS // 2):
                    last = nc.tensor.transpose(gated_bank[i][:, b * P:(b + 1) * P], hgb[:, b, :], ident[:, :])
                last.then_inc(c_T, 1)

            def lora(b):
                i, k = b // (ROWS // 2), b % (ROWS // 2)
                pe.wait_ge(c_lo, i + 1)
                if b < 2:
                    pe.wait_ge(a_add, ROWS - 1 + b)
                else:
                    pe.wait_ge(c_x1, b - 1)
                mm3(bT[b % 2][:, :], [hgT[i][:, a, k * P:(k + 1) * P] for a in range(2)],
                    [lbT[:, a, :] for a in range(2)], True, True).then_inc(c_lora, 1)

            def x1_T(b):
                pe.wait_ge(c_x1, b + 1)
                wait(pe, c_xlo, b - 1)
                for c in range(KT):
                    last = nc.tensor.transpose(halves[b % 2][:, c * P:(c + 1) * P], acc[:, b, c * P:(c + 1) * P],
                                               ident[:, :])
                last.then_inc(c_xT, 1)

            def scores(t, j, h):
                g = 2 * t + j
                if h == 0:
                    pe.wait_ge(kc_lo, g + 1)
                    pe.wait_ge(kn_lo, g + 1)
                    pe.wait_ge(qT_lo, g + 1)
                wait(pe, max_done, 4 * g + h)
                qh = [qT[:, j, a, h, :] for a in range(2)]
                for i in range(2):
                    last = mm3(bS[:, i, :], qh, [kT[:, j, a, i * KEYS // 2:(i + 1) * KEYS // 2] for a in range(2)],
                               True, True)
                last.then_inc(scores_done, 1)

            def k_cache_T(t, j, s):
                n = 2 * t + j + 2
                wait(pe, vn_hi, n)
                if s is not None:
                    pe.wait_ge(wkv_lo, s + 1)
                pe.wait_ge(k_in[j], 16 * CT * (t + 2))
                for c in range(CT):
                    last = nc.tensor.transpose(bK[:, c * P:(c + 1) * P], kraw[:, j, c, :], ident[:, :])
                last.then_inc(kc_done, 1)

            def q_proj(t, j):
                n, m, uses, kv = 2 * t + j + 1, (j + 1) % 2, t + 1 + j, kv_of_next(t, j)
                wait(pe, kn_lo, n)
                if isinstance(n, int) and n < 2:
                    pe.wait_ge(c_xlo, n + 1)
                else:
                    pe.wait_ge(x_in[m], 16 * (uses - 1))
                for c in range(KT):
                    last = mm3(bQ[:, :], [xs[:, m, a, c, :] for a in range(2)],
                               [part_of(wqT, kv, a, c) for a in range(2)], c == 0, c == KT - 1)
                last.then_inc(q_done, 1)

            def kv_proj(t, j, s):
                n, m, kv = 2 * t + j + 1, (j + 1) % 2, kv_of_next(t, j)
                pe.wait_ge(kc_lo, n + 1)
                for c in range(KT):
                    last = mm3(bK[:, 0:2 * HD], [xs[:, m, a, c, :] for a in range(2)],
                               [part_of(wkvT, kv, a, c) for a in range(2)], c == 0, c == KT - 1)
                if s is not None:
                    pe.wait_ge(w_in[0], 48 * (s + 1))
                    for i in range(2):
                        last = nc.tensor.transpose(bK[:, (2 + i) * P:(3 + i) * P],
                                                   wraw[:, 0, QW + i * P:QW + (i + 1) * P], ident[:, :])
                last.then_inc(kv_done, 1)

            def q_T(t, j, on):
                n = 2 * t + j + 1
                pe.wait_ge(qr_ready, n + 1)
                if on:
                    wait(pe, wo_lo if j else wq_lo, t + 1)
                for h in range(REP):
                    last = nc.tensor.transpose(bW[:, h * P:(h + 1) * P], qr[:, h * P:(h + 1) * P], ident[:, :])
                last.then_inc(qT_done, 1)

            def k_new_T(t, j):
                n = 2 * t + j + 1
                pe.wait_ge(kr_ready, n + 1)
                pe.wait_ge(q_copied, n + 1)
                nc.tensor.transpose(bQ[:, 0:P], kr, ident[:, :]).then_inc(kT_done, 1)

            def w_T(t, j, s):
                pe.wait_ge(w_in[1 - j], (16 if j == 0 else 48) * (s + 1))
                pe.wait_ge(qT_lo, 2 * t + j + 2)
                for c in range(4):
                    last = nc.tensor.transpose(bW[:, c * P:(c + 1) * P], wraw[:, 1 - j, c * P:(c + 1) * P], ident[:, :])
                last.then_inc(wqT_done if j else woT_done, 1)

            def probs_T(t, j, k, d=0):
                g = 2 * t + j + d
                wait(pe, p_lo, UNITS * g + k - 1)
                pe.wait_ge(normalised, REP * g + (4 * k + 3) // TILES + 1)
                for i in range(4):
                    tile = 4 * k + i
                    last = nc.tensor.transpose(bT[(j + d + k) % 2][:, i * P:(i + 1) * P],
                                               pr[:, tile // TILES, (tile % TILES) * P:(tile % TILES + 1) * P],
                                               ident[:, :])
                last.then_inc(pT_done, 1)

            def values(t, j):
                f, m = 2 * t + j - 1, (j + 1) % 2
                wait(pe, added, f)
                pe.wait_ge(p_lo, UNITS * f + UNITS)
                pe.wait_ge(vn_split, f + 1)
                pe.wait_ge(vc_split, f + 1)
                for c in range(TILES):
                    last = mm3(bO[:, :], [vs[:, m, a, c, :] for a in range(2)],
                               [pt[:, a, :, c, :] for a in range(2)], c == 0, c == TILES - 1)
                last.then_inc(pv_done, 1)

            def out_proj(t, j):
                f, kv = 2 * t + j - 1, kv_of_last(t, j)
                pe.wait_ge(o_lo, f + 1)
                for h in range(REP):
                    last = mm3(bO[:, :], [ot[:, a, h, :] for a in range(2)],
                               [part_of(woT, kv, a, h) for a in range(2)], h == 0, h == REP - 1)
                last.then_inc(wo_done, 1)

            def turn(t, on=True):
                for j in range(2):
                    this, nxt, prev, after = (there(t, j, d) for d in (0, 1, -1, 2))
                    s = step_of(t, j, on)
                    if this:
                        scores(t, j, 0)
                    if nxt:
                        q_proj(t, j)
                    if this:
                        scores(t, j, 1)
                    if prev:
                        probs_T(t, j, 3, -1)
                        probs_T(t, j, 4, -1)
                    if nxt:
                        kv_proj(t, j, s if j == 1 else None)
                    if this:
                        scores(t, j, 2)
                    if prev:
                        values(t, j)
                    if this:
                        probs_T(t, j, 0)
                        scores(t, j, 3)
                    if nxt:
                        q_T(t, j, on)
                    if this:
                        probs_T(t, j, 1)
                    if prev:
                        out_proj(t, j)
                    if nxt:
                        k_new_T(t, j)
                    if this:
                        probs_T(t, j, 2)
                    if after:
                        k_cache_T(t, j, s if j == 1 else None)
                    if s is not None:
                        w_T(t, j, s)

            x_T(0)
            for i in range(N0):
                prep_unit(i)
            for b in range(ROWS):
                if b + 1 < ROWS:
                    x_T(b + 1)
                if b == ROWS - 1:
                    gated_T(0)
                x_products(b)
                for i in beside_row[b]:
                    prep_unit(i)
            lora(0)
            lora(1)
            x1_T(0)
            x1_T(1)
            k_cache_T(-1, 0, None)
            lora(2)
            lora(3)
            q_proj(-1, 1)
            x1_T(2)
            kv_proj(-1, 1, 0)
            x1_T(3)
            gated_T(1)
            q_T(-1, 1, True)
            k_new_T(-1, 1)
            lora(4)
            lora(5)
            k_cache_T(-1, 1, 0)
            x1_T(4)
            w_T(-1, 1, 0)
            lora(6)
            x1_T(5)
            lora(7)
            x1_T(6)
            x1_T(7)
            pe.wait_ge(c_xlo, ROWS)
            turn(0)
            with pe.Fori(1, STEPS - 1) as t:
                turn(t)
            turn(STEPS - 1)
            with pe.Fori(STEPS, TURNS - 1) as t:
                turn(t, False)
            turn(TURNS - 1, False)
            turn(TURNS, False)

        @block.scalar
        def _(act):
            def take(dst, src):
                return nc.scalar.activation(dst, src, ACT.Copy)

            def prep_take(i):
                _, n, dst = prep[i]
                act.wait_ge(prep_T, i + 1)
                take(dst[0], halves[i % 2][:, 0:KT * n].rearrange("p (t n) -> p t n", t=KT)).then_inc(prep_hi, 1)

            def x_hi(b):
                act.wait_ge(a_T, b + 1)
                wait(act, a_proj, b - 1)
                take(xs[:, b % 2, 0].rearrange("p t n -> p (t n)"), x_bank[b % 2][:, :]).then_inc(a_hi, 1)

            def activations(b):
                act.wait_ge(a_proj, b + 1)
                take(hl[:, b, :], [bQ, bO][b % 2][:, 0:HL]).then_inc(a_hl, 1)

            def second_weight(half_no):
                act.wait_ge(diff_ready, half_no + 1)
                r = slice(half_no * ROWS // 2, (half_no + 1) * ROWS // 2)
                nc.scalar.activation(p2[:, r], m2[:, r], ACT.Exp).then_inc(act_step, 1)

            def gated_hi(i):
                act.wait_ge(c_T, i + 1)
                take(hgT[i][:, 0, :], gated_bank[i]).then_inc(c_hi, 1)

            def x1_hi(b):
                act.wait_ge(c_xT, b + 1)
                if b < 2:
                    act.wait_ge(a_proj, ROWS)
                slot, before = x1_slot(b)
                wait(act, c_out[slot], before)
                take(x1_place(b)[:, 0:DM], halves[b % 2]).then_inc(c_xhi, 1)

            x_hi(0)
            for i in range(N0):
                prep_take(i)
            for b in range(ROWS):
                if b + 1 < ROWS:
                    x_hi(b + 1)
                if b == ROWS - 1:
                    gated_hi(0)
                activations(b)
                for i in beside_row[b]:
                    prep_take(i)
                if b == 1:
                    act.wait_ge(angle_ready, 1)
                    nc.scalar.activation(sint, ang, ACT.Sin).then_inc(sin_ready, 1)
                    act.wait_ge(cosarg_ready, 1)
                    nc.scalar.activation(cost, turns, ACT.Sin).then_inc(cos_ready, 1)
                if b == 5:
                    second_weight(0)

            def k_cache_hi(t, j):
                act.wait_ge(kc_done, 2 * t + j + 3)
                take(kT[:, j, 0, 0:CACHE], bK[:, :]).then_inc(kc_hi, 1)

            def values_cache_hi(t, j):
                m, uses = (j + 1) % 2, t + 1 + j
                act.wait_ge(v_in[m], 16 * CT * uses)
                take(vs[:, m, 0, 0:CT, :], vraw[:, m]).then_inc(vc_hi, 1)

            def q_out(t, j):
                n = 2 * t + j + 1
                act.wait_ge(q_done, n + 1)
                wait(act, q_mul, n)
                take(qs, bQ[:, :]).then_inc(q_copied, 1)

            def q_square(t, j):
                n = 2 * t + j + 1
                act.wait_ge(q_copied, n + 1)
                wait(act, q_summed, n)
                nc.scalar.activation(sq, qs, ACT.Square).then_inc(q_squared, 1)

            def kv_out(t, j):
                n, m = 2 * t + j + 1, (j + 1) % 2
                act.wait_ge(kv_done, n + 1)
                wait(act, k_mul, n)
                wait(act, vn_split, n)
                take(ks, bK[:, 0:2 * HD]).then_inc(kv_copied, 1)
                take(vs[:, m, 0, CT, :], bK[:, HD:2 * HD]).then_inc(vn_hi, 1)

            def k_square(t, j):
                n = 2 * t + j + 1
                act.wait_ge(kv_copied, n + 1)
                wait(act, rk_ready, n)
                nc.scalar.activation(ksq, ks[:, 0:HD], ACT.Square, accum_out=ssk).then_inc(k_squared, 1)

            def exps(t, j, h):
                g = 2 * t + j
                act.wait_ge(bias_ready, 4 * g + h + 1)
                nc.scalar.activation(pr[:, h, :], pr[:, h, :], ACT.Exp, bias=nbias[:, h:h + 1],
                                     scale=rq[:, j, h:h + 1], accum_out=sums[:, h:h + 1]).then_inc(exp_done, 1)

            def normalise(t, j, h, d=0):
                act.wait_ge(rinv_ready, 4 * (2 * t + j + d) + h + 1)
                nc.scalar.activation(pr[:, h, :], pr[:, h, :], ACT.Copy,
                                     scale=rinv[:, h:h + 1]).then_inc(normalised, 1)

            def o_hi_out(t, j):
                act.wait_ge(pv_done, 2 * t + j)
                take(ot[:, 0].rearrange("p h n -> p (h n)"), bO[:, :]).then_inc(o_hi, 1)

            def probs_hi(t, j, k, d=0):
                g = 2 * t + j + d
                act.wait_ge(pT_done, UNITS * g + k + 1)
                take(pt[:, 0].rearrange("p h t n -> p (h t n)")[:, k * 512:(k + 1) * 512],
                     bT[(j + d + k) % 2][:, :]).then_inc(p_hi, 1)

            def q_T_hi(t, j):
                n, m = 2 * t + j + 1, (j + 1) % 2
                act.wait_ge(qT_done, n + 1)
                take(qT[:, m, 0].rearrange("p h n -> p (h n)"), bW[:, :]).then_inc(qT_hi, 1)

            def k_new_hi(t, j):
                n, m = 2 * t + j + 1, (j + 1) % 2
                act.wait_ge(kT_done, n + 1)
                take(kT[:, m, 0, CACHE:KEYS], bQ[:, 0:P]).then_inc(kn_hi, 1)

            def wkv_take(t, s):
                act.wait_ge(kv_done, 2 * t + 3)
                hold(act)
                take(tile_of(wkvT, s, 0), bK[:, 2 * P:4 * P]).then_inc(wkv_hi, 1)

            def w_take(j, s):
                act.wait_ge(wqT_done if j else woT_done, s + 1)
                hold(act)
                take(columns_of(wqT if j else woT, s, 0), bW[:, :].rearrange("p (c n) -> p c n", c=4)).then_inc(
                    wq_hi if j else wo_hi, 1)

            def turn(t, on=True):
                for j in range(2):
                    this, nxt, prev, after = (there(t, j, d) for d in (0, 1, -1, 2))
                    s = step_of(t, j, on)
                    if prev and this:
                        probs_hi(t, j, 2, -1)
                        normalise(t, j, 3, -1)
                    elif prev:
                        normalise(t, j, 3, -1)
                        probs_hi(t, j, 2, -1)
                    if this:
                        exps(t, j, 0)
                    if nxt:
                        q_out(t, j)
                    if prev:
                        probs_hi(t, j, 3, -1)
                        probs_hi(t, j, 4, -1)
                    if nxt:
                        q_square(t, j)
                    if this:
                        exps(t, j, 1)
                        normalise(t, j, 0)
                        normalise(t, j, 1)
                        exps(t, j, 2)
                    if j == 1 and s is not None:
                        wkv_take(t, s)
                    if prev:
                        o_hi_out(t, j)
                    if nxt:
                        kv_out(t, j)
                    if this:
                        probs_hi(t, j, 0)
                    if nxt:
                        k_square(t, j)
                        values_cache_hi(t, j)
                    if this:
                        normalise(t, j, 2)
                    if nxt:
                        q_T_hi(t, j)
                    if this:
                        probs_hi(t, j, 1)
                    if nxt:
                        k_new_hi(t, j)
                    if this:
                        exps(t, j, 3)
                    if s is not None:
                        w_take(j, s)
                    if after:
                        k_cache_hi(t, j)

            x1_hi(0)
            x1_hi(1)
            k_cache_hi(-1, 0)
            act.wait_ge(comp_ready, 8)
            q_out(-1, 1)
            q_square(-1, 1)
            x1_hi(2)
            second_weight(1)
            wkv_take(-1, 0)
            kv_out(-1, 1)
            k_square(-1, 1)
            values_cache_hi(-1, 1)
            x1_hi(3)
            gated_hi(1)
            q_T_hi(-1, 1)
            k_new_hi(-1, 1)
            k_cache_hi(-1, 1)
            x1_hi(4)
            w_take(1, 0)
            x1_hi(5)
            x1_hi(6)
            x1_hi(7)
            for i in range(4):
                act.wait_ge(c_out[2 + i], 32 if i < 2 else 16)
            turn(0)
            with act.Fori(1, STEPS - 1) as t:
                turn(t)
            turn(STEPS - 1)
            with act.Fori(STEPS, TURNS - 1) as t:
                turn(t, False)
            turn(TURNS - 1, False)
            turn(TURNS, False)

        @block.vector
        def _(dve):
            steps = [0]

            def step(ins):
                steps[0] += 1
                ins.then_inc(dve_step, 1)
                dve.wait_ge(dve_step, steps[0])

            def rest(dst, src, hi):
                return nc.vector.tensor_tensor(dst, src, hi.bitcast(FP32), ALU.subtract)

            def prep_rest(i):
                _, n, dst = prep[i]
                dve.wait_ge(prep_hi, i + 1)
                rest(dst[1], halves[i % 2][:, 0:KT * n].rearrange("p (t n) -> p t n", t=KT),
                     dst[0]).then_inc(prep_lo, 1)

            half_hd = HD // 2

            def constants():
                dve.wait_ge(consts_in, 16 * 6)
                dve.wait_ge(const_ready, 1)
                step(nc.vector.tensor_copy(lenf, ints[:, 0:8]))
                nc.vector.tensor_copy(langf, ints[:, 8:16]).then_inc(lens_ready, 1)
                step(nc.vector.tensor_scalar(posf, lenf, tokf, None, ALU.add))

            def page_rows():
                for q in range(4):
                    r = slice(q * PAGE, (q + 1) * PAGE)
                    last = nc.vector.tensor_copy(pageidx[r, :, :],
                                                 tab[r, :].rearrange("p (b c q) -> p b c q", b=ROWS, q=4)[:, :, :, q])
                step(last)
                step(nc.vector.tensor_scalar(pageidx[:, :, :], pageidx[:, :, :], 0.0, 63.0, ALU.max, ALU.min))
                for q in range(4):
                    r = slice(q * PAGE, (q + 1) * PAGE)
                    last = nc.vector.tensor_scalar(pageidx[r, :, :], pageidx[r, :, :], float(PAGE * KVH),
                                                   float(-q * PAGE * KVH), ALU.mult, ALU.add)
                step(last)
                nc.vector.tensor_scalar(pageidx[:, :, :], pageidx[:, :, :], tok8, None, ALU.add).then_inc(idx_step, 1)

            def angles():
                for b in range(ROWS):
                    last = nc.vector.tensor_scalar(ang[:, b * half_hd:(b + 1) * half_hd], sint[:, 0:half_hd],
                                                   posf[:, b:b + 1], None, ALU.mult)
                step(last)
                step(nc.vector.tensor_scalar(turns, ang, 1.0 / TWO_PI, ROUND, ALU.mult, ALU.add))
                step(nc.vector.tensor_scalar(turns, turns, -ROUND, None, ALU.add))

            def remainders():
                for c in two_pi_parts():
                    step(nc.vector.scalar_tensor_tensor(ang, turns, -c, ang, ALU.mult, ALU.add))
                nc.vector.tensor_scalar(ang, ang, 3.1415925, -3.1415925, ALU.min, ALU.max).then_inc(angle_ready, 1)
                dve.wait_ge(angle_ready, 1)
                step(nc.vector.scalar_tensor_tensor(turns, ang, -1.0, ang, ALU.mult, ALU.max))
                nc.vector.tensor_scalar(turns, turns, -1.0, math.pi / 2, ALU.mult, ALU.add).then_inc(cosarg_ready, 1)

            def table_weights():
                nc.vector.tensor_scalar(wn[:, 2, :], wn[:, 2, :], math.sqrt(HD), None, ALU.mult)
                step(nc.vector.tensor_scalar(wn[:, 1, :], wn[:, 0, :], -1.0, None, ALU.mult))
                nc.vector.tensor_copy(wn[:, 1, 0:half_hd], wn[:, 0, 0:half_hd])
                step(nc.vector.tensor_scalar(wn[:, 3, :], wn[:, 2, :], -1.0, None, ALU.mult))
                nc.vector.tensor_copy(wn[:, 3, 0:half_hd], wn[:, 2, 0:half_hd]).then_inc(wn_ready, 1)

            def x_lo(b):
                dve.wait_ge(a_hi, b + 1)
                rest(xs[:, b % 2, 1].rearrange("p t n -> p (t n)"), x_bank[b % 2][:, :],
                     xs[:, b % 2, 0].rearrange("p t n -> p (t n)")).then_inc(a_lo, 1)

            def x_add(b):
                dve.wait_ge(a_proj, b + 1)
                nc.vector.tensor_tensor(acc[:, b, :], bT[b % 2][:, :], acc[:, b, :], ALU.add).then_inc(a_add, 1)

            half_rows = ROWS // 2

            def router(half_no):
                r = slice(half_no * half_rows, (half_no + 1) * half_rows)
                w = slice(r.start * EXPERTS, r.stop * EXPERTS)
                return r, [gwork[:, i, w] for i in range(7)]

            def by_row(v):
                return v.rearrange("p (b e) -> p b e", b=half_rows)

            def wide(v):
                return v.unsqueeze(2).to_broadcast([P, half_rows, EXPERTS])

            def first_largest(half_no, onehot, best):
                r, (lg, eq, _, _, rev, _, _) = router(half_no)
                step(nc.vector.tensor_reduce(best[:, r], by_row(lg), AX.X, ALU.max))
                step(nc.vector.tensor_tensor(by_row(eq), by_row(lg), wide(best[:, r]), ALU.is_equal))
                step(nc.vector.tensor_tensor(eq, eq, rev, ALU.mult))
                step(nc.vector.tensor_reduce(top1[:, r], by_row(eq), AX.X, ALU.max))
                step(nc.vector.tensor_tensor(by_row(onehot), by_row(eq), wide(top1[:, r]), ALU.is_equal))

            def route_first(half_no):
                r, (lg, eq, oh1, _, _, num, _) = router(half_no)
                dve.wait_ge(experts_ready, 1)
                dve.wait_ge(a_hl, r.stop)
                step(nc.vector.tensor_tensor(by_row(eq), by_row(num), wide(langf[:, r]), ALU.is_equal))
                step(nc.vector.scalar_tensor_tensor(by_row(lg), by_row(eq), LANG_BIAS, hl[:, r, ER:HL],
                                                    ALU.mult, ALU.add))
                first_largest(half_no, oh1, m1)

            def route_second(half_no):
                r, (lg, _, oh1, oh2, _, _, _) = router(half_no)
                step(nc.vector.scalar_tensor_tensor(lg, oh1, -3e38, lg, ALU.mult, ALU.add))
                first_largest(half_no, oh2, m2)
                nc.vector.tensor_tensor(m2[:, r], m2[:, r], m1[:, r], ALU.subtract).then_inc(diff_ready, 1)

            def route_gates(half_no):
                r, (_, _, oh1, oh2, _, _, gates) = router(half_no)
                dve.wait_ge(act_step, half_no + 1)
                step(nc.vector.tensor_scalar(p1[:, r], p2[:, r], 1.0, 1.0 / LORA_SCALE, ALU.add, ALU.mult))
                step(nc.vector.reciprocal(p1[:, r], p1[:, r]))
                step(nc.vector.tensor_tensor(p2[:, r], p2[:, r], p1[:, r], ALU.mult))
                nc.vector.tensor_tensor(by_row(oh1), by_row(oh1), wide(p1[:, r]), ALU.mult)
                step(nc.vector.tensor_tensor(by_row(oh2), by_row(oh2), wide(p2[:, r]), ALU.mult))
                step(nc.vector.tensor_tensor(gates, oh1, oh2, ALU.add))

            def gate(i):
                r = slice(i * half_rows, (i + 1) * half_rows)
                wait(dve, c_T, i)
                nc.vector.tensor_tensor(
                    hgb[:, :, :].rearrange("p b (e r) -> p b e r", e=EXPERTS),
                    hl[:, r, 0:ER].rearrange("p b (e r) -> p b e r", e=EXPERTS),
                    by_row(gwork[:, 6, i * half_rows * EXPERTS:(i + 1) * half_rows * EXPERTS]).unsqueeze(3)
                    .to_broadcast([P, half_rows, EXPERTS, RANK]), ALU.mult).then_inc(c_hg, 1)

            def gated_lo(i):
                dve.wait_ge(c_hi, i + 1)
                rest(hgT[i][:, 1, :], gated_bank[i], hgT[i][:, 0, :]).then_inc(c_lo, 1)

            def x1_add(b):
                dve.wait_ge(c_lora, b + 1)
                nc.vector.tensor_tensor(acc[:, b, :], bT[b % 2][:, :], acc[:, b, :], ALU.add).then_inc(c_x1, 1)

            def x1_lo(b):
                dve.wait_ge(c_xhi, b + 1)
                rest(x1_place(b)[:, DM:2 * DM], halves[b % 2], x1_place(b)[:, 0:DM]).then_inc(c_xlo, 1)

            x_lo(0)
            for i in range(N0):
                prep_rest(i)
            for b in range(ROWS):
                if b + 1 < ROWS:
                    x_lo(b + 1)
                if b == ROWS - 1:
                    gated_lo(0)
                x_add(b)
                for i in beside_row[b]:
                    prep_rest(i)
                if b == 0:
                    constants()
                    angles()
                if b == 1:
                    remainders()
                    table_weights()
                if b == 2:
                    page_rows()
                if b == 3:
                    route_first(0)
                if b == 4:
                    route_second(0)
                if b == 5:
                    route_gates(0)
                    gate(0)

            def head_max(t, j, h):
                g = 2 * t + j
                dve.wait_ge(scores_done, 4 * g + h + 1)
                if h == 0:
                    dve.wait_ge(mask_ready, g + 1)
                wait(dve, pT_done, UNITS * (g - 1) + h + 2)
                hold(dve)
                nc.vector.tensor_tensor_reduce(out=pr[:, h, :].rearrange("p (a n) -> p a n", a=2), in0=bS,
                                               in1=mask[:, j, :].rearrange("p (a n) -> p a n", a=2),
                                               scale=1.0, scalar=-3e38,
                                               op0=ALU.add, op1=ALU.max,
                                               accum_out=maxs[:, h:h + 1]).then_inc(max_done, 1)
                dve.wait_ge(max_done, 4 * g + h + 1)
                dve.wait_ge(rq_ready, g + 1)
                nc.vector.scalar_tensor_tensor(nbias[:, h:h + 1], maxs[:, h:h + 1], -1.0, rq[:, j, h:h + 1],
                                               ALU.mult, ALU.mult).then_inc(bias_ready, 1)

            def head_sum(t, j, h, d=0):
                g = 2 * t + j + d
                dve.wait_ge(exp_done, 4 * g + h + 1)
                nc.vector.reciprocal(rinv[:, h:h + 1], sums[:, h:h + 1]).then_inc(rinv_ready, 1)

            def q_add(t, j):
                n, half_hd = 2 * t + j + 1, HD // 2
                a3, b3, r3 = (v.rearrange("p (h n) -> p h n", h=REP) for v in (u1, u2, qr))
                dve.wait_ge(q_mul, n + 1)
                wait(dve, qT_done, n)
                nc.vector.tensor_tensor(r3[:, :, 0:half_hd], a3[:, :, 0:half_hd], b3[:, :, half_hd:HD], ALU.add)
                nc.vector.tensor_tensor(r3[:, :, half_hd:HD], a3[:, :, half_hd:HD], b3[:, :, 0:half_hd],
                                        ALU.add).then_inc(qr_ready, 1)

            def k_cache_lo(t, j):
                n, m = 2 * t + j + 1, (j + 1) % 2
                dve.wait_ge(kc_hi, n + 1)
                rest(kT[:, m, 1, 0:CACHE], bK[:, :], kT[:, m, 0, 0:CACHE]).then_inc(kc_lo, 1)

            def make_mask(t, j):
                n, m, uses = 2 * t + j + 1, (j + 1) % 2, t + 1 + j
                dve.wait_ge(rope_in[m], 16 * uses)
                nc.vector.tensor_scalar(mask[:, m, 0:CACHE], keyno[:, :], rope[:, m, 4 * HD:4 * HD + 1], NEG,
                                        ALU.is_ge, ALU.mult).then_inc(mask_ready, 1)

            def values_cache_lo(t, j):
                dve.wait_ge(vc_hi, 2 * t + j + 1)
                rest(vs[:, j, 1, 0:CT, :], vraw[:, j], vs[:, j, 0, 0:CT, :]).then_inc(vc_split, 1)

            def q_sum(t, j):
                n, m = 2 * t + j + 1, (j + 1) % 2
                dve.wait_ge(q_squared, n + 1)
                nc.vector.tensor_reduce(ssq[:, m, :], sq.rearrange("p (h n) -> p h n", h=REP), AX.X,
                                        ALU.add).then_inc(q_summed, 1)

            def o_lo_out(t, j):
                dve.wait_ge(o_hi, 2 * t + j)
                rest(ot[:, 1].rearrange("p h n -> p (h n)"), bO[:, :],
                     ot[:, 0].rearrange("p h n -> p (h n)")).then_inc(o_lo, 1)

            def probs_lo(t, j, k, d=0):
                g = 2 * t + j + d
                dve.wait_ge(p_hi, UNITS * g + k + 1)
                c = slice(k * 512, (k + 1) * 512)
                rest(pt[:, 1].rearrange("p h t n -> p (h t n)")[:, c], bT[(j + d + k) % 2][:, :],
                     pt[:, 0].rearrange("p h t n -> p (h t n)")[:, c]).then_inc(p_lo, 1)

            def k_rope(t, j):
                n, m = 2 * t + j + 1, (j + 1) % 2
                dve.wait_ge(rk_ready, n + 1)
                wait(dve, kT_done, n)
                nc.vector.scalar_tensor_tensor(kr1, ks[:, 0:HD], rk, rope[:, m, 2 * HD:3 * HD], ALU.mult, ALU.mult)
                nc.vector.scalar_tensor_tensor(kr2, ks[:, 0:HD], rk, rope[:, m, 3 * HD:4 * HD], ALU.mult,
                                               ALU.mult).then_inc(k_mul, 1)
                dve.wait_ge(k_mul, n + 1)
                h = HD // 2
                nc.vector.tensor_tensor(kr[:, 0:h], kr1[:, 0:h], kr2[:, h:HD], ALU.add)
                nc.vector.tensor_tensor(kr[:, h:HD], kr1[:, h:HD], kr2[:, 0:h], ALU.add).then_inc(kr_ready, 1)

            def q_T_lo(t, j):
                n, m = 2 * t + j + 1, (j + 1) % 2
                dve.wait_ge(qT_hi, n + 1)
                rest(qT[:, m, 1].rearrange("p h n -> p (h n)"), bW[:, :],
                     qT[:, m, 0].rearrange("p h n -> p (h n)")).then_inc(qT_lo, 1)

            def add_out(t, j):
                f = 2 * t + j - 1
                dve.wait_ge(wo_done, f + 1)
                row = acc[:, at(f % ROWS), :].rearrange("p a n -> p (a n)")
                nc.vector.tensor_tensor(row, bO[:, :], row, ALU.add).then_inc(added, 1)

            def k_new_lo(t, j):
                n, m = 2 * t + j + 1, (j + 1) % 2
                dve.wait_ge(kn_hi, n + 1)
                rest(kT[:, m, 1, CACHE:KEYS], bQ[:, 0:P], kT[:, m, 0, CACHE:KEYS]).then_inc(kn_lo, 1)

            def wkv_rest(s):
                dve.wait_ge(wkv_hi, s + 1)
                dve.wait_ge(vn_hi, 2 * s + 1)
                rest(tile_of(wkvT, s, 1), bK[:, 2 * P:4 * P], tile_of(wkvT, s, 0)).then_inc(wkv_lo, 1)

            def w_rest(j, s):
                dve.wait_ge(wq_hi if j else wo_hi, s + 1)
                w = wqT if j else woT
                rest(columns_of(w, s, 1), bW[:, :].rearrange("p (c n) -> p c n", c=4),
                     columns_of(w, s, 0)).then_inc(wq_lo if j else wo_lo, 1)

            def turn(t, on=True):
                for j in range(2):
                    this, nxt, prev = (there(t, j, d) for d in (0, 1, -1))
                    s = step_of(t, j, on)
                    if prev and this:
                        head_sum(t, j, 3, -1)
                    if this:
                        head_max(t, j, 0)
                    if prev:
                        probs_lo(t, j, 2, -1)
                    if nxt:
                        k_cache_lo(t, j)
                    if this:
                        head_max(t, j, 1)
                        head_sum(t, j, 0)
                    if prev:
                        probs_lo(t, j, 3, -1)
                        probs_lo(t, j, 4, -1)
                    if this:
                        values_cache_lo(t, j)
                        head_sum(t, j, 1)
                        head_max(t, j, 2)
                    if nxt:
                        q_sum(t, j)
                        q_add(t, j)
                        make_mask(t, j)
                    if this:
                        head_sum(t, j, 2)
                    if prev:
                        o_lo_out(t, j)
                    if this:
                        head_max(t, j, 3)
                        probs_lo(t, j, 0)
                    if nxt:
                        k_rope(t, j)
                    if j == 1 and s is not None:
                        wkv_rest(s)
                    if nxt:
                        q_T_lo(t, j)
                        k_new_lo(t, j)
                    if this:
                        probs_lo(t, j, 1)
                    if this and not nxt:
                        head_sum(t, j, 3)
                    if prev:
                        add_out(t, j)
                    if s is not None:
                        w_rest(j, s)

            x1_add(0)
            x1_add(1)
            x1_lo(0)
            x1_lo(1)
            route_first(1)
            k_cache_lo(-1, 1)
            x1_add(2)
            x1_add(3)
            route_second(1)
            x1_lo(2)
            route_gates(1)
            gate(1)
            q_add(-1, 1)
            k_rope(-1, 1)
            gated_lo(1)
            q_T_lo(-1, 1)
            k_new_lo(-1, 1)
            x1_add(4)
            wkv_rest(0)
            x1_add(5)
            x1_lo(3)
            q_sum(-1, 1)
            x1_lo(4)
            x1_add(6)
            w_rest(1, 0)
            x1_lo(5)
            x1_add(7)
            dve.wait_ge(pool_step, 2)
            make_mask(-1, 1)
            x1_lo(6)
            x1_lo(7)
            turn(0)
            with dve.Fori(1, STEPS - 1) as t:
                turn(t)
            turn(STEPS - 1)
            with dve.Fori(STEPS, TURNS - 1) as t:
                turn(t, False)
            turn(TURNS - 1, False)
            turn(TURNS, False)

        @block.gpsimd
        def _(pool):
            key_rows = kc.rearrange("g s h d -> (g s h) d")
            value_rows = vc.rearrange("g s h d -> (g s h) d")
            nc.gpsimd.iota(tok8, [[0, 1]], base=0, channel_multiplier=KVH, allow_small_or_imprecise_dtypes=True)
            nc.gpsimd.iota(tokf, [[0, 1]], base=0, channel_multiplier=1,
                           allow_small_or_imprecise_dtypes=True).then_inc(const_ready, 1)
            nc.gpsimd.memset(ident[:, :], 0.0).then_inc(pool_step, 1)
            pool.wait_ge(pool_step, 1)
            nc.gpsimd.affine_select(out=ident[:, :], in_=ident[:, :], compare_op=ALU.not_equal, fill=1.0, base=0,
                                    pattern=[[-1, P]], channel_multiplier=1).then_inc(ident_ready, 1)
            nc.gpsimd.memset(half, -0.5)
            nc.gpsimd.memset(one4, 1.0)
            nc.gpsimd.memset(mask[:, :, CACHE:KEYS], 0.0)
            rev, num = gwork[:, 4, :], gwork[:, 5, :]
            nc.gpsimd.iota(rev, [[0, ROWS], [-1, EXPERTS]], base=EXPERTS, channel_multiplier=0,
                           allow_small_or_imprecise_dtypes=True)
            nc.gpsimd.iota(num, [[0, ROWS], [1, EXPERTS]], base=0, channel_multiplier=0,
                           allow_small_or_imprecise_dtypes=True).then_inc(experts_ready, 1)
            def gather_keys(b, j, k):
                gk = 2 * k + j
                pool_row = pageidx[:, at(b), :].rearrange("p a c -> p (a c)")
                wait(pool, idx_step, 1 + 2 * gk)
                wait(pool, kc_done, gk - 1)
                wait(pool, v_in[j], 16 * CT * k)
                hold(pool)
                nc.gpsimd.tensor_copy(kidx[:, j, :], pool_row).then_inc(idx_step, 1)
                wait(pool, idx_step, 2 + 2 * gk)
                hold(pool)
                nc.gpsimd.tensor_tensor(pool_row, pool_row, one4, ALU.add).then_inc(idx_step, 1)
                for c in range(CT):
                    nc.gpsimd.indirect_dma_start(
                        kraw[:, j, c, :], None, key_rows,
                        bass.IndirectOffsetOnAxis(ap=kidx[:, j, c:c + 1], axis=0)).then_inc(k_in[j], 16)

            def gather_values(t, j):
                if there(t, j, 0):
                    pool.wait_ge(vc_split, 2 * t + j + 1)
                    hold(pool)
                for c in range(CT):
                    nc.gpsimd.indirect_dma_start(
                        vraw[:, j, c, :], None, value_rows,
                        bass.IndirectOffsetOnAxis(ap=kidx[:, j, c:c + 1], axis=0)).then_inc(v_in[j], 16)

            def q_tables(t, j):
                n, m, uses = 2 * t + j + 1, (j + 1) % 2, t + 1 + j
                q3, a3, b3 = (v.rearrange("p (h n) -> p h n", h=REP) for v in (qs, u1, u2))
                pool.wait_ge(rope_in[m], 16 * uses)
                pool.wait_ge(q_copied, n + 1)
                wait(pool, qr_ready, n)
                hold(pool)
                nc.gpsimd.tensor_tensor(a3, q3, rope[:, m, 0:HD].unsqueeze(1).to_broadcast([P, REP, HD]), ALU.mult)
                nc.gpsimd.tensor_tensor(b3, q3, rope[:, m, HD:2 * HD].unsqueeze(1).to_broadcast([P, REP, HD]),
                                        ALU.mult).then_inc(q_mul, 1)

            def q_scale(t, j):
                n, m = 2 * t + j + 1, (j + 1) % 2
                pool.wait_ge(q_summed, n + 1)
                hold(pool)
                nc.gpsimd.tensor_scalar(ssq[:, m, :], ssq[:, m, :], HD * EPS, None, ALU.add).then_inc(rq_arg, 1)
                pool.wait_ge(rq_arg, n + 1)
                nc.gpsimd.tensor_tensor(rq[:, m, :], ssq[:, m, :], half, ALU.pow).then_inc(rq_ready, 1)

            def values_new_lo(t, j):
                n, m = 2 * t + j + 1, (j + 1) % 2
                pool.wait_ge(vn_hi, n + 1)
                nc.gpsimd.tensor_tensor(vs[:, m, 1, CT, :], ks[:, HD:2 * HD], vs[:, m, 0, CT, :].bitcast(FP32),
                                        ALU.subtract).then_inc(vn_split, 1)

            def k_scale(t, j):
                n = 2 * t + j + 1
                pool.wait_ge(k_squared, n + 1)
                wait(pool, k_mul, n)
                hold(pool)
                nc.gpsimd.tensor_scalar(ssk1, ssk, HD * EPS, None, ALU.add).then_inc(rk_arg, 1)
                pool.wait_ge(rk_arg, n + 1)
                nc.gpsimd.tensor_tensor(rk, ssk1, half[:, 0:1], ALU.pow).then_inc(rk_ready, 1)

            def turn(t):
                for j in range(2):
                    nxt, after = there(t, j, 1), there(t, j, 2)
                    if after:
                        gather_keys(((t + 1) % PAIRS) * 2 + j, j, t + 1)
                    if nxt:
                        q_tables(t, j)
                    early = isinstance(t, int) and t == 0
                    if after and not early:
                        gather_values(t, j)
                    if nxt:
                        k_scale(t, j)
                        values_new_lo(t, j)
                        q_scale(t, j)
                    if after and early:
                        gather_values(t, j)

            pool.wait_ge(wn_ready, 1)
            pool.wait_ge(sin_ready, 1)
            pool.wait_ge(cos_ready, 1)
            h = HD // 2
            for i in range(8):
                if i >= 2:
                    pool.wait_ge(comp_out[i % 2], 16 * (i // 2))
                wave = (cost, sint)[i // 2 % 2].rearrange("p (b n) -> p b n", b=ROWS)
                weight = wn[:, i // 2, i % 2 * h:(i % 2 + 1) * h]
                nc.gpsimd.tensor_tensor(comp[i % 2], wave, weight.unsqueeze(1).to_broadcast([P, ROWS, h]),
                                        ALU.mult).then_inc(comp_ready, 1)
                if i == 5:
                    pool.wait_ge(prep_T, last_staged[0])
                    gather_keys(0, 0, 0)
            pool.wait_ge(comp_ready, 8)
            nc.gpsimd.iota(keyno[:, :], [[1, CACHE]], base=0, channel_multiplier=0,
                           allow_small_or_imprecise_dtypes=True).then_inc(pool_step, 1)
            pool.wait_ge(prep_T, last_staged[2])
            gather_values(-1, 0)
            pool.wait_ge(prep_T, last_staged[1])
            gather_keys(1, 1, 0)
            pool.wait_ge(prep_T, last_staged[3])
            gather_values(-1, 1)
            q_tables(-1, 1)
            k_scale(-1, 1)
            values_new_lo(-1, 1)
            q_scale(-1, 1)
            turn(0)
            with pool.Fori(1, TURNS - 1) as t:
                turn(t)
            turn(TURNS - 1)


INPUTS = ["x", "itok_B_0_7", "itok_Bx16_0_63", "itok_B_207_1644", "L0_cond_W", "L0_cond_Wr", "L0_cond_A", "L0_cond_B",
          "L1_cond_Wq", "L1_cond_Wk", "L1_cond_Wv", "L1_cond_Wo", "L1_cond_q_norm_w", "L1_cond_k_norm_w",
          "L1_cond_k_cache", "L1_cond_v_cache"]


def kernel(**inputs):
    import concourse.bacc as bacc
    from concourse.bass_utils import run_bass_kernel_spmd

    nc = bacc.Bacc("TRN2", target_bir_lowering=False, num_devices=1)
    arrays, args = {}, []
    for name in INPUTS:
        a = np.ascontiguousarray(inputs[name])
        arrays[f"in_{name}"] = a
        args.append(nc.dram_tensor(f"in_{name}", a.shape, mybir.dt.from_np(a.dtype), kind="ExternalInput").ap())
    inv = (1.0 / 10000.0 ** (np.arange(0, HD, 2, dtype=np.float64) / HD)).astype(np.float32)
    arrays["inv_freq"] = inv
    args.append(nc.dram_tensor("inv_freq", inv.shape, FP32, kind="ExternalInput").ap())
    out = nc.dram_tensor("out", (ROWS, P, DM), FP32, kind="ExternalOutput").ap()
    build(nc, *args, out)
    return run_bass_kernel_spmd(nc, [arrays], core_ids=[0]).results[0]["out"]
```
